# Optimizing a Trainium2 kernel written in Bass

```python
import numpy as np
import jax
import jax.numpy as jnp

def _softmax(x, axis=-1):
    return jax.nn.softmax(x, axis=axis)

def _gelu(x):
    return jax.nn.gelu(x, approximate=True)

def _silu(x):
    return jax.nn.silu(x)

def _sigmoid(x):
    return jax.nn.sigmoid(x)

def _layernorm(x, axis=-1, eps=1e-05):
    m = jnp.mean(x, axis=axis, keepdims=True)
    v = jnp.var(x, axis=axis, keepdims=True)
    return (x - m) / jnp.sqrt(v + eps)

def _scatter_add(tgt, idx, src, axis=0):
    return tgt.at[idx].add(src)

def _segment_sum(src, seg, n):
    return jax.ops.segment_sum(src, seg, n)
kernel_name = 'mk_conv_preact_d4_conv_nchw512_r4_4277fc'

def setup_inputs(seed: int=0):
    np.random.seed(seed)
    _w = jnp.asarray

    def _rec_inputs():
        import jax
        import jax.numpy as jnp
        _gk = jax.random.key(seed)
        x = -8.268e-05 + 0.9999 * jax.random.normal(jax.random.fold_in(_gk, 1), (16, 128, 56, 56), jnp.float32)
        return x
    x = _rec_inputs()

    def _L0_conv_setup():
        import jax, jax.numpy as jnp
        import numpy as np
        EPS = 0.0001
        GROUPS = 8
        N_POWER_ITERS = 19

        def _l2n(v):
            return v / (jnp.linalg.norm(v) + 1e-12)

        def _whiten_subspace(A, v_init):
            L = A.shape[0]

            def step(carry, inputs):
                A, subspace, lam_prev, stopped = carry
                j, v0 = inputs
                v = _l2n(v0)

                def pi(v, _):
                    return (_l2n(A @ v), None)
                v, _ = jax.lax.scan(pi, v, None, length=N_POWER_ITERS)
                Av = A @ v
                lam = v @ Av / (v @ v)
                brk = (j > 0) & ((lam_prev < lam) | (lam < EPS))
                active = ~stopped & ~brk
                lam_safe = jnp.where(active, lam, 1.0)
                vvT = jnp.outer(v, v)
                subspace = subspace + jnp.where(active, jax.lax.rsqrt(lam_safe), 0.0) * vvT
                A = jnp.where(active, A - A @ vvT, A)
                lam_prev = jnp.where(active, lam, lam_prev)
                stopped = stopped | brk
                return ((A, subspace, lam_prev, stopped), None)
            init = (A, jnp.zeros_like(A), jnp.zeros((), A.dtype), jnp.zeros((), bool))
            (_, subspace, _, _), _ = jax.lax.scan(step, init, (jnp.arange(L), v_init))
            return subspace
        key = jax.random.key(seed)
        k1, k2, k3 = jax.random.split(key, 3)
        N, C, H, W = (32, 128, 56, 56)
        L = C // GROUPS
        x = jax.random.normal(k1, (N, C, H, W), dtype=jnp.float32)
        v_init = jax.random.normal(k2, (GROUPS, L, L), dtype=jnp.float32)
        weight = jax.random.uniform(k3, (C, 1), dtype=jnp.float32)
        bias = jnp.zeros((C, 1), dtype=jnp.float32)
        return {'x': x, 'v_init': v_init, 'weight': weight, 'bias': bias}
    _L0_conv_all = _L0_conv_setup()
    _L0_conv_in = {k: v for k, v in _L0_conv_all.items() if k in ('v_init', 'weight', 'bias')}
    del _L0_conv_all

    def _L1_conv_setup():
        import jax, jax.numpy as jnp
        import numpy as np
        C = 128
        G = 16
        Cg = C // G
        K = 3
        P = K * K
        PAD = 1
        STRIDE = 1
        DIL = 1
        DWK = 3
        OFFSET_SCALE = 1.0
        LN_EPS = 1e-05

        def _dcnv3_core(x, offset, mask):
            N, H, W, _ = x.shape
            Hin, Win = (H + 2 * PAD, W + 2 * PAD)
            Hout, Wout = (H, W)
            xpad = jnp.pad(x, ((0, 0), (PAD, PAD), (PAD, PAD), (0, 0)))
            base = DIL * (K - 1) // 2 + 0.5
            ref_y = (base + jnp.arange(Hout, dtype=jnp.float32) * STRIDE) / Hin
            ref_x = (base + jnp.arange(Wout, dtype=jnp.float32) * STRIDE) / Win
            ref = jnp.stack(jnp.broadcast_arrays(ref_x[None, :], ref_y[:, None]), -1)
            g1 = jnp.arange(K, dtype=jnp.float32) * DIL - DIL * (K - 1) // 2
            gxx, gyy = jnp.meshgrid(g1 / Win, g1 / Hin, indexing='ij')
            grid = jnp.stack([gxx, gyy], -1).reshape(P, 2)
            off = offset.reshape(N, Hout, Wout, G, P, 2)
            norm = jnp.array([Win, Hin], jnp.float32)
            loc = ref[None, :, :, None, None, :] + grid * OFFSET_SCALE + off * OFFSET_SCALE / norm
            px = loc[..., 0] * Win - 0.5
            py = loc[..., 1] * Hin - 0.5
            xg = xpad.reshape(N, Hin, Win, G, Cg).transpose(0, 3, 1, 2, 4).reshape(N * G, Hin, Win, Cg)
            pxg = px.transpose(0, 3, 1, 2, 4).reshape(N * G, Hout, Wout, P)
            pyg = py.transpose(0, 3, 1, 2, 4).reshape(N * G, Hout, Wout, P)
            mg = mask.transpose(0, 3, 1, 2, 4).reshape(N * G, Hout, Wout, P)

            def bilin(img, bx, by, m):
                x0 = jnp.floor(bx)
                y0 = jnp.floor(by)
                wx = (bx - x0)[..., None]
                wy = (by - y0)[..., None]
                x0i = x0.astype(jnp.int32)
                y0i = y0.astype(jnp.int32)

                def g(yy, xx):
                    valid = (yy >= 0) & (yy < Hin) & (xx >= 0) & (xx < Win)
                    v = img[jnp.clip(yy, 0, Hin - 1), jnp.clip(xx, 0, Win - 1)]
                    return v * valid[..., None]
                v00 = g(y0i, x0i)
                v01 = g(y0i, x0i + 1)
                v10 = g(y0i + 1, x0i)
                v11 = g(y0i + 1, x0i + 1)
                samp = (v00 * (1 - wx) + v01 * wx) * (1 - wy) + (v10 * (1 - wx) + v11 * wx) * wy
                return jnp.einsum('hwpc,hwp->hwc', samp, m)
            out = jax.vmap(bilin)(xg, pxg, pyg, mg)
            return out.reshape(N, G, Hout, Wout, Cg).transpose(0, 2, 3, 1, 4).reshape(N, Hout, Wout, C)
        key = jax.random.key(seed)
        ks = jax.random.split(key, 10)
        N, H, W = (2, 16, 16)
        sc = 1.0 / np.sqrt(C)
        return {'x': jax.random.normal(ks[0], (N, C, H, W), jnp.float32), 'dw_w': jax.random.normal(ks[1], (C, 1, DWK, DWK), jnp.float32) * 0.1, 'dw_b': jax.random.normal(ks[2], (C,), jnp.float32) * 0.02, 'ln_g': jnp.ones((C,), jnp.float32), 'ln_b': jnp.zeros((C,), jnp.float32), 'off_w': jax.random.normal(ks[3], (C, G * P * 2), jnp.float32) * 0.01, 'off_b': jax.random.normal(ks[4], (G * P * 2,), jnp.float32) * 0.01, 'mask_w': jax.random.normal(ks[5], (C, G * P), jnp.float32) * 0.01, 'mask_b': jnp.zeros((G * P,), jnp.float32), 'in_w': jax.random.normal(ks[6], (C, C), jnp.float32) * sc, 'in_b': jnp.zeros((C,), jnp.float32), 'out_w': jax.random.normal(ks[7], (C, C), jnp.float32) * sc, 'out_b': jnp.zeros((C,), jnp.float32)}
    _L1_conv_all = _L1_conv_setup()
    _L1_conv_in = {k: v for k, v in _L1_conv_all.items() if k in ('dw_w', 'dw_b', 'ln_g', 'ln_b', 'off_w', 'off_b', 'mask_w', 'mask_b', 'in_w', 'in_b', 'out_w', 'out_b')}
    del _L1_conv_all

    def _L2_conv_setup():
        import jax, jax.numpy as jnp
        import numpy as np
        HEADS = 16
        DIM_HEAD = 32
        WSZ = 7
        DIM = 128
        INNER = HEADS * DIM_HEAD
        LN_EPS = 1e-05
        key = jax.random.key(seed)
        ks = jax.random.split(key, 9)
        b, H, W = (16, 56, 56)
        x = jax.random.normal(ks[0], (b, DIM, H, W), dtype=jnp.float32)
        w_qkv = jax.random.normal(ks[1], (INNER * 3, DIM), dtype=jnp.float32) * DIM ** (-0.5)
        window_tokens = jax.random.normal(ks[2], (DIM,), dtype=jnp.float32)
        ln_w = jnp.ones((DIM_HEAD,), dtype=jnp.float32)
        ln_b = jnp.zeros((DIM_HEAD,), dtype=jnp.float32)
        w_qk = jax.random.normal(ks[3], (INNER * 2, INNER), dtype=jnp.float32) * INNER ** (-0.5)
        b_qk = jnp.zeros((INNER * 2,), dtype=jnp.float32)
        w_out = jax.random.normal(ks[4], (DIM, INNER), dtype=jnp.float32) * INNER ** (-0.5)
        b_out = jnp.zeros((DIM,), dtype=jnp.float32)
        return {'x': x, 'w_qkv': w_qkv, 'window_tokens': window_tokens, 'ln_w': ln_w, 'ln_b': ln_b, 'w_qk': w_qk, 'b_qk': b_qk, 'w_out': w_out, 'b_out': b_out}
    _L2_conv_all = _L2_conv_setup()
    _L2_conv_in = {k: v for k, v in _L2_conv_all.items() if k in ('w_qkv', 'window_tokens', 'ln_w', 'ln_b', 'w_qk', 'b_qk', 'w_out', 'b_out')}
    del _L2_conv_all

    def _L3_conv_setup():
        import jax, jax.numpy as jnp
        import numpy as np
        from jax import lax

        def _get_mu(x):
            bs, depth, h, w = x.shape
            ix = jnp.arange(1, h + 1, dtype=x.dtype).reshape(1, 1, h, 1)
            iy = jnp.arange(1, w + 1, dtype=x.dtype).reshape(1, 1, 1, w)
            sumX = jnp.maximum(x.sum((2, 3)), 1e-09)
            mu_x = jnp.maximum(jnp.round((ix * x).sum((2, 3)) / sumX), 1.0)
            mu_y = jnp.maximum(jnp.round((iy * x).sum((2, 3)) / sumX), 1.0)
            lin = jnp.linspace(-1.0, 1.0, h, dtype=x.dtype)
            mu_xg = lin[(mu_x - 1.0).astype(jnp.int32)]
            mu_yg = lin[(mu_y - 1.0).astype(jnp.int32)]
            return (mu_xg, mu_yg)

        def _get_mask(x, mask_weight, filt):
            bs, depth, h, w = x.shape
            mu_x, mu_y = _get_mu(x)
            posX = jnp.linspace(-1.0, 1.0, h, dtype=x.dtype).reshape(1, 1, h, 1)
            posY = jnp.linspace(-1.0, 1.0, w, dtype=x.dtype).reshape(1, 1, 1, w)
            m = jnp.abs(posX - mu_x[:, :, None, None]) + jnp.abs(posY - mu_y[:, :, None, None])
            m = 1.0 - m * mask_weight.reshape(1, depth, 1, 1)
            m = jnp.maximum(m, -1.0)
            m = jnp.where(filt.reshape(1, depth, 1, 1) == 1.0, m, 1.0)
            return m
        key = jax.random.key(seed)
        k1, k2, k3, k4 = jax.random.split(key, 4)
        bs, depth, h, w = (32, 128, 28, 28)
        out_c, kh, kw = (128, 3, 3)
        x = jax.random.uniform(k1, (bs, depth, h, w), dtype=jnp.float32)
        weight = jax.random.normal(k2, (out_c, depth, kh, kw), dtype=jnp.float32) * 0.02
        bias = jax.random.normal(k3, (out_c,), dtype=jnp.float32) * 0.02
        mask_weight = jax.random.uniform(k4, (depth,), dtype=jnp.float32)
        filt = jnp.ones((depth, 1), dtype=jnp.float32)
        return {'x': x, 'weight': weight, 'bias': bias, 'mask_weight': mask_weight, 'filter': filt, 'padding': 1}
    _L3_conv_all = _L3_conv_setup()
    _L3_conv_in = {k: v for k, v in _L3_conv_all.items() if k in ('weight', 'bias', 'mask_weight', 'filter')}
    del _L3_conv_all
    return {'x': x, 'L0_conv_v_init': _L0_conv_in['v_init'], 'L0_conv_weight': _L0_conv_in['weight'], 'L0_conv_bias': _L0_conv_in['bias'], 'L1_conv_dw_w': _L1_conv_in['dw_w'], 'L1_conv_dw_b': _L1_conv_in['dw_b'], 'L1_conv_ln_g': _L1_conv_in['ln_g'], 'L1_conv_ln_b': _L1_conv_in['ln_b'], 'L1_conv_off_w': _L1_conv_in['off_w'], 'L1_conv_off_b': _L1_conv_in['off_b'], 'L1_conv_mask_w': _L1_conv_in['mask_w'], 'L1_conv_mask_b': _L1_conv_in['mask_b'], 'L1_conv_in_w': _L1_conv_in['in_w'], 'L1_conv_in_b': _L1_conv_in['in_b'], 'L1_conv_out_w': _L1_conv_in['out_w'], 'L1_conv_out_b': _L1_conv_in['out_b'], 'L2_conv_w_qkv': _L2_conv_in['w_qkv'], 'L2_conv_window_tokens': _L2_conv_in['window_tokens'], 'L2_conv_ln_w': _L2_conv_in['ln_w'], 'L2_conv_ln_b': _L2_conv_in['ln_b'], 'L2_conv_w_qk': _L2_conv_in['w_qk'], 'L2_conv_b_qk': _L2_conv_in['b_qk'], 'L2_conv_w_out': _L2_conv_in['w_out'], 'L2_conv_b_out': _L2_conv_in['b_out'], 'L3_conv_weight': _L3_conv_in['weight'], 'L3_conv_bias': _L3_conv_in['bias'], 'L3_conv_mask_weight': _L3_conv_in['mask_weight'], 'L3_conv_filter': _L3_conv_in['filter']}

def reference(x, L0_conv_v_init, L0_conv_weight, L0_conv_bias, L1_conv_dw_w, L1_conv_dw_b, L1_conv_ln_g, L1_conv_ln_b, L1_conv_off_w, L1_conv_off_b, L1_conv_mask_w, L1_conv_mask_b, L1_conv_in_w, L1_conv_in_b, L1_conv_out_w, L1_conv_out_b, L2_conv_w_qkv, L2_conv_window_tokens, L2_conv_ln_w, L2_conv_ln_b, L2_conv_w_qk, L2_conv_b_qk, L2_conv_w_out, L2_conv_b_out, L3_conv_weight, L3_conv_bias, L3_conv_mask_weight, L3_conv_filter):
    import jax
    import jax.numpy as jnp

    def _L0_conv_ref(x, v_init, weight, bias):
        import jax, jax.numpy as jnp
        import numpy as np
        EPS = 0.0001
        GROUPS = 8
        N_POWER_ITERS = 19

        def _l2n(v):
            return v / (jnp.linalg.norm(v) + 1e-12)

        def _whiten_subspace(A, v_init):
            L = A.shape[0]

            def step(carry, inputs):
                A, subspace, lam_prev, stopped = carry
                j, v0 = inputs
                v = _l2n(v0)

                def pi(v, _):
                    return (_l2n(A @ v), None)
                v, _ = jax.lax.scan(pi, v, None, length=N_POWER_ITERS)
                Av = A @ v
                lam = v @ Av / (v @ v)
                brk = (j > 0) & ((lam_prev < lam) | (lam < EPS))
                active = ~stopped & ~brk
                lam_safe = jnp.where(active, lam, 1.0)
                vvT = jnp.outer(v, v)
                subspace = subspace + jnp.where(active, jax.lax.rsqrt(lam_safe), 0.0) * vvT
                A = jnp.where(active, A - A @ vvT, A)
                lam_prev = jnp.where(active, lam, lam_prev)
                stopped = stopped | brk
                return ((A, subspace, lam_prev, stopped), None)
            init = (A, jnp.zeros_like(A), jnp.zeros((), A.dtype), jnp.zeros((), bool))
            (_, subspace, _, _), _ = jax.lax.scan(step, init, (jnp.arange(L), v_init))
            return subspace
        N, C, H, W = x.shape
        G = GROUPS
        L = C // G
        M = N * H * W
        xc = x.transpose(1, 0, 2, 3).reshape(C, M)
        mu = xc.mean(axis=1, keepdims=True)
        xc = xc - mu
        xg = xc.reshape(G, L, M)
        cov = jnp.einsum('gim,gjm->gij', xg, xg) / M + EPS * jnp.eye(L, dtype=xc.dtype)
        subspaces = jax.vmap(_whiten_subspace)(cov, v_init)
        xgr = jnp.einsum('gij,gjm->gim', subspaces, xg)
        xr = xgr.reshape(C, M) * weight + bias
        return xr.reshape(C, N, H, W).transpose(1, 0, 2, 3)

    def _L1_conv_ref(x, dw_w, dw_b, ln_g, ln_b, off_w, off_b, mask_w, mask_b, in_w, in_b, out_w, out_b):
        import jax, jax.numpy as jnp
        import numpy as np
        C = 128
        G = 16
        Cg = C // G
        K = 3
        P = K * K
        PAD = 1
        STRIDE = 1
        DIL = 1
        DWK = 3
        OFFSET_SCALE = 1.0
        LN_EPS = 1e-05

        def _dcnv3_core(x, offset, mask):
            N, H, W, _ = x.shape
            Hin, Win = (H + 2 * PAD, W + 2 * PAD)
            Hout, Wout = (H, W)
            xpad = jnp.pad(x, ((0, 0), (PAD, PAD), (PAD, PAD), (0, 0)))
            base = DIL * (K - 1) // 2 + 0.5
            ref_y = (base + jnp.arange(Hout, dtype=jnp.float32) * STRIDE) / Hin
            ref_x = (base + jnp.arange(Wout, dtype=jnp.float32) * STRIDE) / Win
            ref = jnp.stack(jnp.broadcast_arrays(ref_x[None, :], ref_y[:, None]), -1)
            g1 = jnp.arange(K, dtype=jnp.float32) * DIL - DIL * (K - 1) // 2
            gxx, gyy = jnp.meshgrid(g1 / Win, g1 / Hin, indexing='ij')
            grid = jnp.stack([gxx, gyy], -1).reshape(P, 2)
            off = offset.reshape(N, Hout, Wout, G, P, 2)
            norm = jnp.array([Win, Hin], jnp.float32)
            loc = ref[None, :, :, None, None, :] + grid * OFFSET_SCALE + off * OFFSET_SCALE / norm
            px = loc[..., 0] * Win - 0.5
            py = loc[..., 1] * Hin - 0.5
            xg = xpad.reshape(N, Hin, Win, G, Cg).transpose(0, 3, 1, 2, 4).reshape(N * G, Hin, Win, Cg)
            pxg = px.transpose(0, 3, 1, 2, 4).reshape(N * G, Hout, Wout, P)
            pyg = py.transpose(0, 3, 1, 2, 4).reshape(N * G, Hout, Wout, P)
            mg = mask.transpose(0, 3, 1, 2, 4).reshape(N * G, Hout, Wout, P)

            def bilin(img, bx, by, m):
                x0 = jnp.floor(bx)
                y0 = jnp.floor(by)
                wx = (bx - x0)[..., None]
                wy = (by - y0)[..., None]
                x0i = x0.astype(jnp.int32)
                y0i = y0.astype(jnp.int32)

                def g(yy, xx):
                    valid = (yy >= 0) & (yy < Hin) & (xx >= 0) & (xx < Win)
                    v = img[jnp.clip(yy, 0, Hin - 1), jnp.clip(xx, 0, Win - 1)]
                    return v * valid[..., None]
                v00 = g(y0i, x0i)
                v01 = g(y0i, x0i + 1)
                v10 = g(y0i + 1, x0i)
                v11 = g(y0i + 1, x0i + 1)
                samp = (v00 * (1 - wx) + v01 * wx) * (1 - wy) + (v10 * (1 - wx) + v11 * wx) * wy
                return jnp.einsum('hwpc,hwp->hwc', samp, m)
            out = jax.vmap(bilin)(xg, pxg, pyg, mg)
            return out.reshape(N, G, Hout, Wout, Cg).transpose(0, 2, 3, 1, 4).reshape(N, Hout, Wout, C)
        N, _, H, W = x.shape
        inp = jnp.transpose(x, (0, 2, 3, 1))
        xproj = inp @ in_w + in_b
        x1 = jax.lax.conv_general_dilated(x, dw_w, (1, 1), [((DWK - 1) // 2, (DWK - 1) // 2)] * 2, feature_group_count=C, dimension_numbers=('NCHW', 'OIHW', 'NCHW'))
        x1 = jnp.transpose(x1, (0, 2, 3, 1)) + dw_b
        mu = x1.mean(-1, keepdims=True)
        var = ((x1 - mu) ** 2).mean(-1, keepdims=True)
        x1 = (x1 - mu) / jnp.sqrt(var + LN_EPS) * ln_g + ln_b
        x1 = jax.nn.gelu(x1, approximate=False)
        offset = x1 @ off_w + off_b
        mask = jax.nn.softmax((x1 @ mask_w + mask_b).reshape(N, H, W, G, P), -1)
        out = _dcnv3_core(xproj, offset, mask)
        out = out @ out_w + out_b
        return jnp.transpose(out, (0, 3, 1, 2))

    def _L2_conv_ref(x, w_qkv, window_tokens, ln_w, ln_b, w_qk, b_qk, w_out, b_out):
        import jax, jax.numpy as jnp
        import numpy as np
        HEADS = 16
        DIM_HEAD = 32
        WSZ = 7
        DIM = 128
        INNER = HEADS * DIM_HEAD
        LN_EPS = 1e-05
        b, c, H, W = x.shape
        h, d, wsz = (HEADS, DIM_HEAD, WSZ)
        X, Y = (H // wsz, W // wsz)
        nw = X * Y
        n = wsz * wsz
        scale = d ** (-0.5)
        xw = x.reshape(b, c, X, wsz, Y, wsz).transpose(0, 2, 4, 1, 3, 5).reshape(b * nw, c, n)
        wt = jnp.broadcast_to(window_tokens[None, :, None], (b * nw, c, 1))
        xc = jnp.concatenate([wt, xw], axis=-1)
        qkv = jnp.einsum('oc,bcn->bon', w_qkv, xc)
        q, k, v = jnp.split(qkv, 3, axis=1)

        def to_heads(t):
            return t.reshape(t.shape[0], h, d, n + 1).transpose(0, 1, 3, 2)
        q, k, v = (to_heads(q), to_heads(k), to_heads(v))
        dots = jnp.einsum('bhid,bhjd->bhij', q * scale, k)
        attn = jax.nn.softmax(dots, axis=-1)
        out = jnp.einsum('bhij,bhjd->bhid', attn, v)
        wtok = out[:, :, 0].reshape(b, nw, h, d).transpose(0, 2, 1, 3)
        wfm = out[:, :, 1:].reshape(b, nw, h, n, d).transpose(0, 2, 1, 3, 4)
        mu = wtok.mean(-1, keepdims=True)
        var = wtok.var(-1, keepdims=True)
        normed = (wtok - mu) / jnp.sqrt(var + LN_EPS) * ln_w + ln_b
        g = jax.nn.gelu(normed, approximate=False)
        gf = g.transpose(0, 1, 3, 2).reshape(b, h * d, nw)
        qk = jnp.einsum('oc,bcn->bon', w_qk, gf) + b_qk[None, :, None]
        qk = qk.reshape(b, h, 2 * d, nw).transpose(0, 1, 3, 2)
        w_q, w_k = (qk[..., :d], qk[..., d:])
        w_dots = jnp.einsum('bhid,bhjd->bhij', w_q * scale, w_k)
        w_attn = jax.nn.softmax(w_dots, axis=-1)
        agg = jnp.einsum('bhij,bhjnd->bhind', w_attn, wfm)
        fmap = agg.reshape(b, h, X, Y, wsz, wsz, d).transpose(0, 1, 6, 2, 4, 3, 5).reshape(b, h * d, H, W)
        return jnp.einsum('oc,bchw->bohw', w_out, fmap) + b_out[None, :, None, None]

    def _L3_conv_ref(x, weight, bias, mask_weight, filter, padding):
        import jax, jax.numpy as jnp
        import numpy as np
        from jax import lax

        def _get_mu(x):
            bs, depth, h, w = x.shape
            ix = jnp.arange(1, h + 1, dtype=x.dtype).reshape(1, 1, h, 1)
            iy = jnp.arange(1, w + 1, dtype=x.dtype).reshape(1, 1, 1, w)
            sumX = jnp.maximum(x.sum((2, 3)), 1e-09)
            mu_x = jnp.maximum(jnp.round((ix * x).sum((2, 3)) / sumX), 1.0)
            mu_y = jnp.maximum(jnp.round((iy * x).sum((2, 3)) / sumX), 1.0)
            lin = jnp.linspace(-1.0, 1.0, h, dtype=x.dtype)
            mu_xg = lin[(mu_x - 1.0).astype(jnp.int32)]
            mu_yg = lin[(mu_y - 1.0).astype(jnp.int32)]
            return (mu_xg, mu_yg)

        def _get_mask(x, mask_weight, filt):
            bs, depth, h, w = x.shape
            mu_x, mu_y = _get_mu(x)
            posX = jnp.linspace(-1.0, 1.0, h, dtype=x.dtype).reshape(1, 1, h, 1)
            posY = jnp.linspace(-1.0, 1.0, w, dtype=x.dtype).reshape(1, 1, 1, w)
            m = jnp.abs(posX - mu_x[:, :, None, None]) + jnp.abs(posY - mu_y[:, :, None, None])
            m = 1.0 - m * mask_weight.reshape(1, depth, 1, 1)
            m = jnp.maximum(m, -1.0)
            m = jnp.where(filt.reshape(1, depth, 1, 1) == 1.0, m, 1.0)
            return m
        mask = _get_mask(x, mask_weight, filter)
        x_relu = jnp.maximum(x * mask, 0.0)
        out = lax.conv_general_dilated(x_relu, weight, window_strides=(1, 1), padding=[(padding, padding), (padding, padding)], dimension_numbers=('NCHW', 'OIHW', 'NCHW'))
        return out + bias.reshape(1, -1, 1, 1)

    def _gn(v, G=32, eps=1e-05):
        B_, C_, H_, W_ = v.shape
        g = v.reshape(B_, G, C_ // G, H_, W_)
        m = jnp.mean(g, axis=(2, 3, 4), keepdims=True)
        s = jnp.var(g, axis=(2, 3, 4), keepdims=True)
        return ((g - m) / jnp.sqrt(s + eps)).reshape(v.shape)

    def _ln_c(v, eps=1e-06):
        m = jnp.mean(v, axis=1, keepdims=True)
        s = jnp.var(v, axis=1, keepdims=True)
        return (v - m) / jnp.sqrt(s + eps)

    def _ln_t(v, eps=1e-05):
        m = jnp.mean(v, axis=-1, keepdims=True)
        s = jnp.var(v, axis=-1, keepdims=True)
        return (v - m) / jnp.sqrt(s + eps)

    def _to_tokens(v):
        B_, C_, H_, W_ = v.shape
        return v.reshape(B_, C_, H_ * W_).transpose(0, 2, 1)

    def _from_tokens(t, like):
        B_, C_, H_, W_ = like.shape
        return t.transpose(0, 2, 1).reshape(B_, C_, H_, W_)
    x = x + _L0_conv_ref(_gn(x), L0_conv_v_init, L0_conv_weight, L0_conv_bias)
    x = x + _L1_conv_ref(_gn(x), L1_conv_dw_w, L1_conv_dw_b, L1_conv_ln_g, L1_conv_ln_b, L1_conv_off_w, L1_conv_off_b, L1_conv_mask_w, L1_conv_mask_b, L1_conv_in_w, L1_conv_in_b, L1_conv_out_w, L1_conv_out_b)
    x = x + _L2_conv_ref(_gn(x), L2_conv_w_qkv, L2_conv_window_tokens, L2_conv_ln_w, L2_conv_ln_b, L2_conv_w_qk, L2_conv_b_qk, L2_conv_w_out, L2_conv_b_out)
    x = x + _L3_conv_ref(_gn(x), L3_conv_weight, L3_conv_bias, L3_conv_mask_weight, L3_conv_filter, 1)
    return x

_drawn_inputs = setup_inputs


def setup_inputs(seed=0):
    import zlib

    import numpy as np

    out = dict(_drawn_inputs(seed))
    spreads = {'L0_conv_bias': (0.0, 0.1),
     'L1_conv_ln_g': (1.0, 0.6),
     'L1_conv_ln_b': (0.0, 0.8),
     'L1_conv_in_b': (0.0, 0.1),
     'L1_conv_out_b': (0.0, 0.1),
     'L2_conv_ln_w': (1.0, 0.6),
     'L2_conv_ln_b': (0.0, 0.8),
     'L2_conv_b_qk': (0.0, 0.8),
     'L2_conv_b_out': (0.0, 0.1),
     'L3_conv_filter': (1.0, 0.2)}
    factors = {'L1_conv_dw_b': 8.0,
     'L1_conv_off_b': 8.0,
     'L1_conv_mask_w': 3.04,
     'L2_conv_window_tokens': 2.852,
     'L2_conv_w_qk': 5.363,
     'L3_conv_bias': 3.525}
    for name, (base, spread) in spreads.items():
        noise = np.random.default_rng([zlib.crc32(name.encode()), seed]).standard_normal(out[name].shape)
        drawn = base * np.exp(spread * noise) if base else spread * noise
        out[name] = jnp.asarray(drawn.astype(out[name].dtype))
    for name, factor in factors.items():
        out[name] = (out[name] * factor).astype(out[name].dtype)
    return out
```

```python
from contextlib import ExitStack

import concourse.bass as bass
from concourse import mybir

F32 = mybir.dt.float32
I32 = mybir.dt.int32
ALU = mybir.AluOpType
ACT = mybir.ActivationFunctionType
AX = mybir.AxisListType

N, C, H, W = 16, 128, 56, 56
PIX = H * W
GN_EPS = 1e-5
LN_EPS = 1e-5
EPS0 = 1e-4
GROUPS0 = 8
L = C // GROUPS0
G1, P9, CG = 16, 9, 8
ROWS = 8
CHUNKS = H // ROWS
CH = ROWS * W
HALF = W // 2
PP = 2 * H
TILES = HALF
T4 = 4
TCH = TILES // T4
NH, DH, WS = 16, 32, 7
NWY = W // WS
NTOK = WS * WS + 1
SLOT = 64
INNER = NH * DH
SCALE = float(DH) ** -0.5
SHIFTS = 5
IMGX = HALF + 4
OFFS = 3 * P9 * G1
POW_D, POW_P = 9, 9
ACT_SMP, ACT_CHK = 1, 1
DVE_A, DVE_COV, DVE_POW, DVE_SMP, DVE_CHK = 20, 12, 22, 34, 22
MAGIC = 12582912.0
TINY = 1e-37

PRIME = 1


class Signal:

    def __init__(self, sem, per):
        self.sem, self.per = sem, per

    def after(self, n):
        return n + PRIME

    def at(self, i, k=None):
        return i * self.per + (self.per if k is None else k) + PRIME


class Chain:

    def __init__(self, eng, sem):
        self.eng, self.sem, self.base, self.n = eng, sem, 0, 0

    def turn(self, i, per):
        if self.n:
            assert self.per == self.n, (self.per, self.n)
        self.base, self.n, self.per = i * per, 0, per

    def end(self):
        assert self.per == self.n, (self.sem, self.per, self.n)

    def step(self, ins):
        ins.then_inc(self.sem, 1)
        self.n += 1
        self.eng.wait_ge(self.sem, self.base + self.n)


def build(nc, a):
    with ExitStack() as ctx:
        def sb(name, shape, dt=F32):
            return ctx.enter_context(nc.sbuf_tensor(name, shape, dt))

        def sem(name):
            return ctx.enter_context(nc.semaphore(name))

        cst = sb("cst", [C, 4, C])
        ident, mask16, gavg, mean128 = (cst[:, k, :] for k in range(4))
        posidx = sb("posidx", [C, 2, W])
        pos, idx = posidx[:, 0, :], posidx[:, 1, :]
        inw = sb("inw", [C, C])
        outw = sb("outw", [C, C])
        offw = sb("offw", [C, OFFS])
        dwdiag = sb("dwdiag", [C, P9, C])
        wqk = sb("wqk", [C, 2 * INNER])
        wv = sb("wv", [C, INNER])
        wqk2 = sb("wqk2", [C, 4, 2 * INNER])
        wout = sb("wout", [C, 4, C])
        convw = sb("convw", [C, 9, C])
        inb_row = sb("inb_row", [PP, C])
        offb_row = sb("offb_row", [PP, OFFS])
        lnw_row = sb("lnw_row", [C, 2, DH])
        cols = sb("cols", [C, 32])
        b0, dwb, lng, lnb, outb, bout, cb, mw, filt, wtok = (cols[:, k:k + 1] for k in range(10))
        dww = cols[:, 10:19]
        bqk = cols[:, 19:27]
        keep = cols[:, 27:28]
        neg_mw = cols[:, 28:29]
        floor2 = cols[:, 29:30]
        w0 = sb("w0", [C, C])
        w0s = sb("w0s", [C, C])
        r0 = sb("r0", [C, N])
        q0 = sb("q0", [C, N])
        mu0 = sb("mu0", [C, 1])
        eps_col = sb("eps_col", [C, 1])
        mvs = sb("mvs", [C, CHUNKS, 6])
        sm = sb("sm", [C, 48])
        x = sb("x", [C, PIX])
        vp = sb("vp", [C, H + 2, W + 2])
        x_yx = x[:, :].rearrange("c (h w) -> c h w", h=H)
        x_tile = x[:, :].rearrange("c (p k t) -> c k t p", k=TCH, t=T4)
        x_win = x[:, :].rearrange("c (X i Y j) -> c X i Y j", X=NWY, i=WS, Y=NWY, j=WS)
        vp_in = vp[:, 1:H + 1, 1:W + 1]
        IMG = SHIFTS * IMGX * C
        HN = P9 * T4 * G1
        HATS_AT = IMG + PIX + T4 * PP + 3 * HN
        ARENA = HATS_AT + 6 * HN + 2 * HN + 25 * T4 * G1 + 5 * T4 * C + 2 * T4 * PP + 2 * T4 * G1
        arena = sb("arena", [C, ARENA])

        def carver(start=0):
            at = [start]

            def carve(n):
                v = arena[:, at[0]:at[0] + n]
                at[0] += n
                assert at[0] <= ARENA, at[0]
                return v
            return carve

        cv = carver()
        xt = [cv(TILES * (C + 1)).rearrange("p (t c) -> p t c", t=TILES) for _ in range(2)]
        gs = [cv(C + 1) for _ in range(2)]
        gdr = [cv(C) for _ in range(2)]
        cacc, junk = cv(C), cv(C)
        st0 = [cv(2) for _ in range(2)]
        gm0 = [cv(6) for _ in range(2)]
        u0, wu0 = cv(N), cv(N)
        colT, rowT = cv(3 * C), cv(2 * C)
        aat, bbt, b2, b4 = cv(2 * C), cv(2 * C), cv(2 * C + 1), cv(C + 1)
        vi = cv(L)
        uw, uwp = cv(2), cv(2)
        ubw, uwm = cv(2 * C), cv(2 * C)
        smat, w0row = cv(C), cv(C)
        it = cv(24)
        cv = carver()
        img = cv(IMG).rearrange("p (a x c) -> p a x c", a=SHIFTS, x=IMGX)
        y1 = cv(PIX)
        gc = cv(T4 * PP)
        om = cv(3 * HN)
        hat = cv(6 * HN).rearrange("p (a c n) -> p a c n", a=3, c=2)
        tt = [cv(HN) for _ in range(2)]
        kw = cv(25 * T4 * G1)
        prod = cv(5 * T4 * C).rearrange("p (k n) -> p k n", k=5)
        dc = cv(T4 * PP)
        res1 = cv(T4 * PP)
        mx1 = cv(T4 * G1)
        sx1 = cv(T4 * G1)
        cv = carver(HATS_AT)
        sq = [cv(CH) for _ in range(2)]
        sd = cv(PIX)
        y1_tile = y1.rearrange("c (p k t) -> c k t p", k=TCH, t=T4)
        cv = carver()
        QW = NWY * NTOK + SLOT - NTOK
        xwb = cv(NWY * SLOT).rearrange("p (w s) -> p w s", w=NWY)
        qk = cv(8 * QW).rearrange("p (m n) -> p m n", m=8)
        v_sb = [cv(NH * (DH + 1)).rearrange("p (h d) -> p h d", h=NH) for _ in range(4)]
        ss = [cv(NH * NTOK) for _ in range(2)]
        e_sb = [cv(NH * C).rearrange("p (o j) -> p o j", o=NH) for _ in range(2)]
        et = [cv(NH * C) for _ in range(2)]
        o_sb = [cv(INNER) for _ in range(2)]
        wf = cv(NTOK * INNER // 2).rearrange("p (n c) -> p n c", n=NTOK)
        at2 = cv(8 * C)
        a2 = cv(8 * C).rearrange("p (h w) -> p h w", h=8)
        ag = cv(4 * WS * SLOT).rearrange("p (m n) -> p m n", m=4)
        yt = cv(WS * SLOT)
        mxs = [cv(NH) for _ in range(2)]
        rec = [cv(NH) for _ in range(2)]
        cv = carver(NWY * SLOT)
        tok, tok2 = cv(8 * DH), cv(8 * DH)
        gfT = cv(4 * SLOT).rearrange("p (m w) -> p m w", m=4)
        qk2 = cv(8 * SLOT).rearrange("p (m w) -> p m w", m=8)
        s2 = cv(8 * SLOT)
        t8 = [cv(8) for _ in range(6)]
        cv = carver(HATS_AT)
        mk = cv(PIX).rearrange("p (h w) -> p h w", h=H)
        axy, rsum, rtmp = cv(2 * W), cv(2 * W), cv(2 * W)

        ps = ctx.enter_context(nc.psum_tensor("ps", [C, 8, 512], F32))

        signals = []

        def sig(name, per=1):
            signals.append(Signal(sem(name), per))
            return signals[-1]

        s_w = sem("weights_loaded")
        s_init = sem("init_done")
        s_passed = sem("waits_passed")
        s_dw = sem("dwdiag_built")
        d_init, d_a, d_cov, d_pow, d_smp, d_chk, d_blk, d_end = (sem(f"dve_own_{k}") for k in range(8))
        t_smp, t_chk = sem("act_own_sample"), sem("act_own_chunk")
        a_xt = [sig("a_xt0", 16), sig("a_xt1", 16)]
        a_gram = [sig("a_gram0"), sig("a_gram1")]
        a_cols, a_gm, a_var, a_sd = sig("a_cols"), sig("a_gm"), sig("a_var"), sig("a_sd")
        a_dr, a_scaled = sig("a_dr"), sig("a_scaled")
        c_d, c_p = sem("cov_dve"), sem("cov_pe")
        p_d, p_p = sig("pow_dve", POW_D), sig("pow_pe", POW_P)
        p_ls, p_sd = sig("pow_lambda"), sig("pow_sqrt")
        s_w0 = sem("w0_ready")
        x_in, x_out = sig("x_in", 16), sig("x_out", 16)
        l0_w, l0_c, l0_y = sig("l0_weights"), sig("l0_const"), sig("l0_psum", CHUNKS)
        gn_st, gn_gm, gn_var, gn_sd, gn_ab = (sig(f"gn_{k}", 3) for k in ("stats", "group", "var", "sd", "ab"))
        v1_in = sig("v1_in")
        xp_p, xp_s = sig("xproj_psum", TCH), sig("xproj_sbuf", TCH)
        z_img = sig("images_zeroed")
        cp_img = sig("images_shifted", 14 * 16)
        dw_p, dw_s = sig("dw_psum", CHUNKS), sig("dw_sbuf", CHUNKS)
        ln_m, ln_c, ln_q, ln_v, ln_s, ln_y = (sig(f"ln_{k}", CHUNKS) for k in
                                              ("mean", "centred", "square", "var", "sd", "normed"))
        gc_s, of_p, of_s, mk_m, mk_e, ht_s = (sig(k) for k in ("gelu_chunk", "off_psum", "off_sbuf", "mask_shifted",
                                                               "mask_exp", "hats"))
        k_z, k_s = sig("taps_zeroed"), sig("taps_built")
        pr_s, pr_u = sig("prod_ready", 25), sig("prod_used", 25)
        dc_s, oo_p, rs_s, rs_a = sig("dc_sbuf"), sig("out1_psum"), sig("res1_sbuf"), sig("res1_added")
        l2_z, xw_s = sig("l2_zeroed", 7), sig("xwin")
        qk_p, qk_a, qk_d = sig("qk_psum", 8), sig("qk_sbuf_act", 4), sig("qk_sbuf_dve", 4)
        s_p, s_s, v_p, v_s, ex_s = sig("s_psum", 4), sig("s_shifted", 4), sig("v_psum", 4), sig("v_sbuf", 4), sig("exps", 4)
        tr_p, tr_a, tr_d = sig("et_psum", 16), sig("et_sbuf_act", 8), sig("et_sbuf_dve", 8)
        pv_p, o_s = sig("pv_psum", 4), sig("o_sbuf", 4)
        wf_in = [sig("wf_in0", 2 * 64), sig("wf_in1", 2 * 64)]
        (tk_v, tk_sd, tk_s, tk_g, gt_p, gt_s, q2_p, q2_s, s2_p, s2_m, s2_e, a2_s, a2_p, a2_t) = (
            sig(k) for k in ("tok_var", "tok_sd", "tok_normed", "tok_gelu", "gft_psum", "gft_sbuf", "qk2_psum",
                             "qk2_sbuf", "s2_psum", "s2_shifted", "s2_exp", "a2_sbuf", "a2t_psum", "a2t_sbuf"))
        ag_p, ag_a, ag_d = sig("agg_psum", WS), sig("agg_act", WS), sig("agg_dve", WS)
        y2_p, y2_e, y2_s = sig("y2_psum", WS), sig("y2_sbuf", WS), sig("y2_added", WS)
        v3_s, mk_s, rl_s = sig("v3"), sig("masked"), sig("relu")
        c3_p, c3_s = sig("conv_psum", CHUNKS), sig("conv_added", CHUNKS)

        block = ctx.enter_context(nc.Block())
        WEIGHTS = 17 * 16
        INITS = 6

        def alone(eng):
            eng.sem_inc(s_passed, 1)

        def heads():
            return [(r * 4 + m, 4 * m + r, m, r) for m in range(4) for r in range(4)]

        def heads2():
            return [(r * 2 + kk, hh, kk, r) for hh in range(2) for kk in range(2) for r in range(4)]

        @block.sync
        def _(sp):
            loads = [(cst[:, :, :], a["c_mats"]), (posidx[:, :, :], a["c_pos"]), (cols[:, 0:27], a["cols"]),
                     (vi, a["v_init"]), (w0row, a["w0_row"].partition_broadcast(C)),
                     (inw[:, :], a["in_w"]), (outw[:, :], a["out_w"]), (offw[:, :], a["offm_w"]),
                     (wqk[:, :], a["wqk"]), (wv[:, :], a["wv"]), (wqk2[:, :, :], a["wqk2"]),
                     (wout[:, :, :], a["wout"]), (convw[:, :, :], a["convw"]),
                     (inb_row[:, :], a["in_b"].partition_broadcast(PP)),
                     (offb_row[:, :], a["offm_b"].partition_broadcast(PP)),
                     (lnw_row[:, 0, :], a["ln2_w"].partition_broadcast(C)),
                     (lnw_row[:, 1, :], a["ln2_b"].partition_broadcast(C))]
            for dst, src in loads:
                sp.dma_start(dst, src).then_inc(s_w, 16)
            with sp.Fori(0, N // 2) as i:
                for u in range(2):
                    sp.wait_ge(a_gram[u].sem, a_gram[u].after(i))
                    sp.dma_start(xt[u][0:PP, :, 0:C], a["x_t"][bass.ds(i * 2 + u, 1)].rearrange(
                        "a (p t) c -> p (a t) c", t=TILES)).then_inc(a_xt[u].sem, 16)
            with sp.Fori(0, N) as i:
                sp.wait_ge(x_out.sem, x_out.at(i, 0))
                sp.dma_start(x[:, :], a["x"][bass.ds(i, 1)].rearrange("a c n -> c (a n)")).then_inc(x_in.sem, 16)
                sp.wait_ge(xp_s.sem, xp_s.at(i))
                for s in (2, 0, 1, 3, 4):
                    d = s - 2
                    lo, hi = max(0, -d), H - max(0, d)
                    if d:
                        sp.dma_start(img[2 * lo:2 * hi, s, 2:2 + HALF, :],
                                     img[2 * (lo + d):2 * (hi + d), 2, 2:2 + HALF, :]).then_inc(cp_img.sem, 16)
                    sp.dma_start(img[2 * lo:2 * hi:2, s, 2 + HALF:, :],
                                 img[2 * (lo + d) + 1:2 * (hi + d):2, 2, 2:4, :]).then_inc(cp_img.sem, 16)
                    sp.dma_start(img[2 * lo + 1:2 * hi:2, s, 0:2, :],
                                 img[2 * (lo + d):2 * (hi + d):2, 2, HALF:HALF + 2, :]).then_inc(cp_img.sem, 16)
                for b in range(NWY):
                    for pr in range(4):
                        sp.wait_ge(o_s.sem, o_s.after(i * NWY * 4 + b * 4 + pr + 1))
                        for wi in range(2):
                            for hh in range(2):
                                w = b * NWY + 2 * pr + wi
                                sp.dma_start(wf[hh * SLOT + w:hh * SLOT + w + 1, :, :],
                                             o_sb[pr % 2][wi * SLOT:wi * SLOT + NTOK, hh * 256:(hh + 1) * 256]
                                             ).then_inc(wf_in[pr % 2].sem, 16)
                sp.wait_ge(c3_s.sem, c3_s.at(i))
                sp.dma_start(a["out"][bass.ds(i, 1)].rearrange("a c n -> c (a n)"), x[:, :]).then_inc(x_out.sem, 16)
            sp.wait_ge(x_out.sem, x_out.at(N, 0))

        @block.gpsimd
        def _(pool):
            for sg in signals:
                pool.sem_inc(sg.sem, PRIME)
            for u in range(2):
                nc.gpsimd.memset(xt[u][0:PP, :, C:C + 1], 1.0).then_inc(s_init, 1)
            nc.gpsimd.memset(cacc, 0.0).then_inc(s_init, 1)
            nc.gpsimd.memset(smat, 0.0).then_inc(s_init, 1)
            nc.gpsimd.memset(vp[:, :, :], 0.0).then_inc(s_init, 1)
            nc.gpsimd.memset(eps_col[:, :], GN_EPS).then_inc(s_init, 1)
            pool.wait_ge(s_w0, 1)
            with pool.Fori(0, N) as i:
                pool.wait_ge(y2_s.sem, y2_s.at(i, 0))
                alone(pool)
                nc.gpsimd.memset(img[0:PP, :, :, :].rearrange("p a x c -> p (a x c)"), 0.0).then_inc(z_img.sem, 1)
                pool.wait_ge(c3_s.sem, c3_s.at(i, 0))
                alone(pool)
                with pool.Fori(0, TCH) as c:
                    ic = i * TCH + c
                    pool.wait_ge(pr_s.sem, pr_s.after(ic * 25))
                    pool.wait_ge(ln_y.sem, ln_y.at(i))
                    alone(pool)
                    nc.gpsimd.memset(kw[0:PP, :], 0.0).then_inc(k_z.sem, 1)
                    pool.wait_ge(rs_s.sem, rs_s.after(ic + 1))
                    alone(pool)
                    xv = x_tile[:, bass.ds(c, 1), :, :].rearrange("c k t p -> c (k t) p")
                    nc.gpsimd.tensor_tensor(xv, xv, res1.rearrange("c (t p) -> c t p", t=T4), ALU.add
                                            ).then_inc(rs_a.sem, 1)
                pool.wait_ge(rs_a.sem, rs_a.at(i * TCH + TCH, 0))
                pool.wait_ge(oo_p.sem, oo_p.after((i + 1) * TCH))
                alone(pool)
                nc.gpsimd.memset(xwb, 0.0).then_inc(l2_z.sem, 1)
                nc.gpsimd.memset(qk, 0.0).then_inc(l2_z.sem, 1)
                for u in range(4):
                    nc.gpsimd.memset(v_sb[u], 1.0)
                for u in range(2):
                    nc.gpsimd.memset(e_sb[u], 0.0).then_inc(l2_z.sem, 1)
                nc.gpsimd.memset(a2, 0.0).then_inc(l2_z.sem, 3)
                for nb in range(WS):
                    pool.wait_ge(y2_e.sem, y2_e.at(i, nb + 1))
                    alone(pool)
                    xv = x_win[:, :, nb, :, :]
                    yv = yt.rearrange("c (j X Y) -> c X Y j", j=WS, X=NWY)
                    nc.gpsimd.tensor_tensor(xv, xv, yv, ALU.add).then_inc(y2_s.sem, 1)

        def gn_group(pe, i, g):
            o = 10 * g
            pe.wait_ge(gn_st.sem, gn_st.at(i, g + 1))
            nc.tensor.matmul(ps[:, 7, 0:2], gavg, sm[:, o:o + 2], start=True, stop=True).then_inc(gn_gm.sem, 1)

        def conv3(pe, k, weights, done):
            for tap in range(9):
                dy, dx = tap // 3, tap % 3
                mm = nc.tensor.matmul(ps[:, k, 0:CH], weights[:, tap, :],
                                      vp[:, ROWS * k + dy:ROWS * k + dy + ROWS, dx:dx + W],
                                      start=(tap == 0), stop=(tap == 8))
            mm.then_inc(done.sem, 1)

        @block.tensor
        def _(pe):
            pe.wait_ge(s_init, INITS)
            pe.wait_ge(s_w, WEIGHTS)
            with pe.Fori(0, N // 2) as i:
                for u in range(2):
                    pe.wait_ge(a_xt[u].sem, a_xt[u].at(i))
                    pe.wait_ge(a_dr.sem, a_dr.after(i * 2))
                    for t in range(TILES):
                        mm = nc.tensor.matmul(ps[:, u, 0:C + 1], xt[u][0:PP, t, 0:C], xt[u][0:PP, t, :],
                                              start=(t == 0), stop=(t == TILES - 1))
                    mm.then_inc(a_gram[u].sem, 1)
                for u in range(2):
                    pe.wait_ge(a_cols.sem, a_cols.after(i * 2 + u + 1))
                    nc.tensor.matmul(ps[:, 2, 0:2], gavg, st0[u], start=True, stop=True).then_inc(a_gm.sem, 1)
                    pe.wait_ge(a_dr.sem, a_dr.after(i * 2 + u + 1))
                    nc.tensor.matmul(ps[:, 3, 0:C], gs[u][:, 0:C], gdr[u], start=True, stop=True
                                     ).then_inc(a_scaled.sem, 1)
            pe.wait_ge(c_d, 1)
            for k, v in enumerate((u0, q0[:, :], wu0)):
                nc.tensor.transpose(ps[0:N, 4, k * C:(k + 1) * C], v, ident)
            nc.tensor.transpose(ps[0:1, 4, 3 * C:4 * C], mu0[:, :], ident).then_inc(c_p, 1)
            pe.wait_ge(c_d, 2)
            nc.tensor.matmul(ps[:, 5, 0:C], colT[0:N, 0:C], rowT[0:N, 0:C], start=True, stop=False)
            nc.tensor.matmul(ps[:, 5, 0:C], colT[0:N, C:2 * C], colT[0:N, 2 * C:3 * C], start=False, stop=False)
            nc.tensor.matmul(ps[:, 5, 0:C], junk[0:1, :], rowT[0:1, C:2 * C], start=False, stop=True).then_inc(c_p, 1)
            with pe.Fori(0, L) as j:
                n = [0]

                def after(k=1):
                    n[0] += k
                    pe.wait_ge(p_d.sem, p_d.at(j, n[0]))

                after()
                nc.tensor.matmul(ps[:, 0, 0:1], mask16, it[:, 0:1], start=True, stop=True).then_inc(p_p.sem, 1)
                after()
                nc.tensor.matmul(ps[:, 1, 0:C], bbt[:, C:], bbt[:, 0:C], start=True, stop=True)
                nc.tensor.matmul(ps[:, 1, C:2 * C], bbt[:, 0:C], bbt[:, C:], start=True, stop=True)
                nc.tensor.matmul(ps[:, 1, 2 * C:2 * C + 1], bbt[:, C:], it[:, 20:21], start=True, stop=True
                                 ).then_inc(p_p.sem, 1)
                after()
                nc.tensor.matmul(ps[:, 2, 0:C], b2[:, 0:C], b2[:, C:2 * C], start=True, stop=True)
                nc.tensor.matmul(ps[:, 2, C:C + 1], b2[:, C:2 * C], b2[:, 2 * C:], start=True, stop=True
                                 ).then_inc(p_p.sem, 1)
                after()
                for k in range(4):
                    if k:
                        after()
                    nc.tensor.matmul(ps[:, 3, k:k + 1], b4[:, 0:C], b4[:, C:] if k == 0 else it[:, 1:2],
                                     start=True, stop=True).then_inc(p_p.sem, 1)
                after()
                nc.tensor.matmul(ps[:, 3, 4:5], aat[:, C:], uw[:, 0:1], start=True, stop=True).then_inc(p_p.sem, 1)
                after()
                nc.tensor.matmul(ps[:, 4, 0:C], ubw[:, 0:C], ident, start=True, stop=True)
                nc.tensor.matmul(ps[:, 4, C:2 * C], ubw[:, C:], ident, start=True, stop=True)
                nc.tensor.matmul(ps[:, 5, 0:2], mask16, uwp, start=True, stop=True).then_inc(p_p.sem, 1)
                assert n[0] == POW_D
            with pe.Fori(0, N) as i:
                pe.wait_ge(l0_w.sem, l0_w.at(i))
                pe.wait_ge(x_in.sem, x_in.at(i))
                pe.wait_ge(c3_s.sem, c3_s.at(i, 0))
                nc.tensor.matmul(ps[:, 7, 8:9], w0[:, :], sm[:, 30:31], start=True, stop=True).then_inc(l0_c.sem, 1)
                for k in range(CHUNKS):
                    nc.tensor.matmul(ps[:, k, 0:CH], w0s[:, :], x[:, k * CH:(k + 1) * CH], start=True, stop=True
                                     ).then_inc(l0_y.sem, 1)
                gn_group(pe, i, 0)
                pe.wait_ge(v1_in.sem, v1_in.at(i))
                for k in range(TCH):
                    for t in range(T4):
                        mm = nc.tensor.matmul(ps[0:PP, k, t * C:(t + 1) * C],
                                              sd.rearrange("c (p x) -> c x p", x=HALF)[:, k * T4 + t, :], inw[:, :],
                                              start=True, stop=True)
                    mm.then_inc(xp_p.sem, 1)
                for k in range(CHUNKS):
                    pe.wait_ge(xp_s.sem, xp_s.at(i, k + 1))
                    conv3(pe, k, dwdiag, dw_p)
                for k in range(CHUNKS):
                    pe.wait_ge(dw_s.sem, dw_s.at(i, k + 1))
                    nc.tensor.matmul(ps[:, k, 0:CH], mean128, y1[:, k * CH:(k + 1) * CH], start=True, stop=True
                                     ).then_inc(ln_m.sem, 1)
                for k in range(CHUNKS):
                    pe.wait_ge(ln_q.sem, ln_q.at(i, k + 1))
                    nc.tensor.matmul(ps[:, k, 0:CH], mean128, sq[k % 2], start=True, stop=True).then_inc(ln_v.sem, 1)
                pe.wait_ge(ln_s.sem, ln_s.at(i))
                alone(pe)
                with pe.Fori(0, TCH) as c:
                    ic = i * TCH + c
                    pe.wait_ge(gc_s.sem, gc_s.after(ic + 1))
                    pe.wait_ge(of_s.sem, of_s.after(ic))
                    for t in range(T4):
                        mm = nc.tensor.matmul(ps[0:PP, t, 0:OFFS], gc[:, t * PP:(t + 1) * PP], offw[:, :],
                                              start=True, stop=True)
                    mm.then_inc(of_p.sem, 1)
                    pe.wait_ge(dc_s.sem, dc_s.after(ic))
                    for s in range(25):
                        pe.wait_ge(pr_s.sem, pr_s.after(ic * 25 + s + 1))
                        for t in range(T4):
                            mm = nc.tensor.matmul(ps[:, 4, t * PP:(t + 1) * PP], prod[0:PP, s % 5, t * C:(t + 1) * C],
                                                  ident[0:PP, 0:PP], start=(s == 0 and t == 0),
                                                  stop=(s == 24 and t == T4 - 1), skip_group_check=True)
                        mm.then_inc(pr_u.sem, 1)
                    pe.wait_ge(dc_s.sem, dc_s.after(ic + 1))
                    pe.wait_ge(rs_s.sem, rs_s.after(ic))
                    nc.tensor.matmul(ps[:, 5, 0:T4 * PP], outw[:, :], dc, start=True, stop=True).then_inc(oo_p.sem, 1)
                gn_group(pe, i, 1)
                with pe.Fori(0, NWY) as b:
                    ib = i * NWY + b

                    def scores(pr):
                        pe.wait_ge(s_s.sem, s_s.after(ib * 4 + pr))
                        for o, h, m, r in heads():
                            for wi in range(2):
                                w = (2 * pr + wi) * NTOK
                                mm = nc.tensor.matmul(ps[wi * SLOT:(wi + 1) * SLOT, r, m * NTOK:(m + 1) * NTOK],
                                                      qk[32 * r:32 * r + 32, m, w:w + SLOT],
                                                      qk[32 * r:32 * r + 32, 4 + m, w:w + NTOK],
                                                      start=True, stop=True, skip_group_check=True)
                        mm.then_inc(s_p.sem, 1)

                    pe.wait_ge(xw_s.sem, xw_s.after(ib + 1))
                    pe.wait_ge(tr_a.sem, tr_a.at(ib, 0))
                    pe.wait_ge(tr_d.sem, tr_d.at(ib, 0))
                    pe.wait_ge(rs_s.sem, rs_s.after((i + 1) * TCH))
                    for m in range(8):
                        if m >= 2:
                            own = qk_a if m % 2 == 0 else qk_d
                            pe.wait_ge(own.sem, own.at(ib, m // 2))
                        nc.tensor.matmul(ps[:, 4 + m % 2, 0:NWY * NTOK], wqk[:, m * C:(m + 1) * C], xwb[:, :, 0:NTOK],
                                         start=True, stop=True).then_inc(qk_p.sem, 1)
                    pe.wait_ge(o_s.sem, o_s.at(ib, 0))
                    for pr in range(4):
                        if pr >= 2:
                            pe.wait_ge(v_s.sem, v_s.at(ib, pr - 1))
                        nc.tensor.matmul(ps[:, 6 + pr % 2, :], xwb[:, 2 * pr:2 * pr + 2, :], wv[:, :],
                                         start=True, stop=True).then_inc(v_p.sem, 1)
                    pe.wait_ge(qk_a.sem, qk_a.at(ib))
                    pe.wait_ge(qk_d.sem, qk_d.at(ib))
                    scores(0)
                    pe.wait_ge(v_s.sem, v_s.at(ib))
                    for pr in range(4):
                        u = pr % 2
                        if pr < 3:
                            scores(pr + 1)
                        pe.wait_ge(ex_s.sem, ex_s.at(ib, pr + 1))
                        for q in range(4):
                            own = tr_a if q % 2 == 0 else tr_d
                            pe.wait_ge(own.sem, own.at(ib, pr * 2 + q // 2))
                            for k in range(4):
                                mm = nc.tensor.transpose(ps[:, 4 + q % 2, k * C:(k + 1) * C], e_sb[u][:, 4 * q + k, :],
                                                         ident)
                            mm.then_inc(tr_p.sem, 1)
                        pe.wait_ge(tr_a.sem, tr_a.at(ib, pr * 2 + 2))
                        pe.wait_ge(tr_d.sem, tr_d.at(ib, pr * 2 + 2))
                        pe.wait_ge(o_s.sem, o_s.at(ib, pr))
                        for o, h, m, r in heads():
                            mm = nc.tensor.matmul(ps[:, 6 + h // 8, (h % 8) * (DH + 1):(h % 8 + 1) * (DH + 1)],
                                                  et[u][:, o * C:(o + 1) * C], v_sb[pr][:, h, :],
                                                  start=True, stop=True, skip_group_check=True)
                        mm.then_inc(pv_p.sem, 1)
                pe.wait_ge(tk_g.sem, tk_g.at(i))
                for kk in range(2):
                    mm = nc.tensor.transpose(ps[:, 0, kk * C:(kk + 1) * C], tok[:, kk * C:(kk + 1) * C], ident)
                mm.then_inc(gt_p.sem, 1)
                pe.wait_ge(gt_s.sem, gt_s.at(i))
                for oc in range(8):
                    for kc in range(4):
                        mm = nc.tensor.matmul(ps[:, 1, oc * SLOT:(oc + 1) * SLOT], wqk2[:, kc, oc * C:(oc + 1) * C],
                                              gfT[:, kc, :], start=(kc == 0), stop=(kc == 3), skip_group_check=True)
                mm.then_inc(q2_p.sem, 1)
                pe.wait_ge(q2_s.sem, q2_s.at(i))
                for o, hh, kk, r in heads2():
                    m = 2 * hh + kk
                    mm = nc.tensor.matmul(ps[hh * SLOT:(hh + 1) * SLOT, r, kk * SLOT:(kk + 1) * SLOT],
                                          qk2[32 * r:32 * r + 32, m, :], qk2[32 * r:32 * r + 32, 4 + m, :],
                                          start=True, stop=True, skip_group_check=True)
                mm.then_inc(s2_p.sem, 1)
                pe.wait_ge(a2_s.sem, a2_s.at(i))
                for o in range(8):
                    mm = nc.tensor.transpose(ps[:, 4 + o // 4, (o % 4) * C:(o % 4 + 1) * C], a2[:, o, :], ident)
                mm.then_inc(a2_p.sem, 1)
                pe.wait_ge(a2_t.sem, a2_t.at(i))
                alone(pe)

                def aggregate(nb):
                    if nb:
                        pe.wait_ge(ag_a.sem, ag_a.at(i, nb))
                        pe.wait_ge(ag_d.sem, ag_d.at(i, nb))
                        alone(pe)
                    for j in range(WS):
                        for o, hh, kk, r in heads2():
                            c0 = (4 * kk + r) * DH
                            mm = nc.tensor.matmul(ps[32 * r:32 * r + 32, 2 * hh + kk, j * SLOT:(j + 1) * SLOT],
                                                  wf[hh * SLOT:(hh + 1) * SLOT, 1 + nb * WS + j, c0:c0 + DH],
                                                  at2[hh * SLOT:(hh + 1) * SLOT, o * C + hh * SLOT:o * C + (hh + 1) * SLOT],
                                                  start=True, stop=True, skip_group_check=True)
                    mm.then_inc(ag_p.sem, 1)

                aggregate(0)
                for nb in range(WS):
                    pe.wait_ge(ag_a.sem, ag_a.at(i, nb + 1))
                    pe.wait_ge(ag_d.sem, ag_d.at(i, nb + 1))
                    if nb >= 2:
                        pe.wait_ge(y2_e.sem, y2_e.at(i, nb - 1))
                    for m in range(4):
                        mm = nc.tensor.matmul(ps[:, 4 + nb % 2, 0:WS * SLOT], wout[:, m, :], ag[:, m, :],
                                              start=(m == 0), stop=(m == 3))
                    mm.then_inc(y2_p.sem, 1)
                    if nb + 1 < WS:
                        aggregate(nb + 1)
                gn_group(pe, i, 2)
                pe.wait_ge(rl_s.sem, rl_s.at(i))
                for k in range(CHUNKS):
                    conv3(pe, k, convw, c3_p)

        def gn_sqrt(act, i, g):
            o = 10 * g
            act.wait_ge(gn_var.sem, gn_var.at(i, g + 1))
            nc.scalar.activation(sm[:, o + 7:o + 8], sm[:, o + 6:o + 7], ACT.Sqrt, bias=eps_col[:, :], scale=-1.0
                                 ).then_inc(gn_sd.sem, 1)

        @block.scalar
        def _(act):
            act.wait_ge(s_init, INITS)
            act.wait_ge(s_w, WEIGHTS)
            alone(act)
            with act.Fori(0, N // 2) as i:
                for u in range(2):
                    act.wait_ge(a_var.sem, a_var.after(i * 2 + u + 1))
                    nc.scalar.activation(gm0[u][:, 3:4], gm0[u][:, 2:3], ACT.Sqrt, bias=eps_col[:, :], scale=-1.0
                                         ).then_inc(a_sd.sem, 1)
            with act.Fori(0, L) as j:
                act.wait_ge(p_ls.sem, p_ls.at(j))
                nc.scalar.activation(it[:, 12:13], it[:, 11:12], ACT.Sqrt).then_inc(p_sd.sem, 1)
            own, ownc = Chain(act, t_smp), Chain(act, t_chk)
            with act.Fori(0, N) as i:
                own.turn(i, ACT_SMP)
                gn_sqrt(act, i, 0)
                act.wait_ge(gn_ab.sem, gn_ab.at(i, 1))
                act.wait_ge(pr_s.sem, pr_s.at(i * TCH, 0))
                nc.scalar.activation(sd, x[:, :], ACT.Identity, bias=sm[:, 9:10], scale=sm[:, 8:9])
                nc.scalar.activation(vp_in, x_yx, ACT.Identity, bias=sm[:, 9:10], scale=sm[:, 8:9]
                                     ).then_inc(v1_in.sem, 1)
                for k in range(CHUNKS):
                    act.wait_ge(dw_p.sem, dw_p.at(i, k + 1))
                    nc.scalar.activation(y1[:, k * CH:(k + 1) * CH], ps[:, k, 0:CH], ACT.Identity, bias=dwb
                                         ).then_inc(dw_s.sem, 1)
                for k in range(CHUNKS):
                    act.wait_ge(ln_c.sem, ln_c.at(i, k + 1))
                    if k >= 2:
                        act.wait_ge(ln_v.sem, ln_v.at(i, k - 1))
                    nc.scalar.activation(sq[k % 2], y1[:, k * CH:(k + 1) * CH], ACT.Square).then_inc(ln_q.sem, 1)
                for k in range(CHUNKS):
                    act.wait_ge(ln_v.sem, ln_v.at(i, k + 1))
                    nc.scalar.activation(sd[:, k * CH:(k + 1) * CH], ps[:, k, 0:CH], ACT.Sqrt, bias=eps_col[:, :]
                                         ).then_inc(ln_s.sem, 1)
                for k in range(CHUNKS):
                    act.wait_ge(ln_y.sem, ln_y.at(i, k + 1))
                    ins = nc.scalar.activation(y1[:, k * CH:(k + 1) * CH], y1[:, k * CH:(k + 1) * CH], ACT.Gelu,
                                               bias=lnb, scale=lng)
                own.step(ins)
                with act.Fori(0, TCH) as c:
                    ic = i * TCH + c
                    ownc.turn(ic, ACT_CHK)
                    act.wait_ge(of_p.sem, of_p.after(ic))
                    nc.scalar.activation(gc.rearrange("c (t p) -> c t p", t=T4),
                                         y1_tile[:, bass.ds(c, 1), :, :].rearrange("c k t p -> c (k t) p"), ACT.Copy
                                         ).then_inc(gc_s.sem, 1)
                    act.wait_ge(of_s.sem, of_s.after(ic + 1))
                    act.wait_ge(k_s.sem, k_s.after(ic))
                    nc.scalar.activation(hat[0:PP, 2, :, :].rearrange("p c n -> p (c n)"), om[0:PP, 0:2 * HN], ACT.Relu)
                    nc.scalar.activation(hat[0:PP, 0, :, :].rearrange("p c n -> p (c n)"), om[0:PP, 0:2 * HN], ACT.Relu,
                                         scale=-1.0)
                    ownc.step(nc.scalar.activation(hat[0:PP, 1, :, :].rearrange("p c n -> p (c n)"), om[0:PP, 0:2 * HN],
                                                   ACT.Abs))
                    nc.scalar.activation(hat[0:PP, 1, :, :].rearrange("p c n -> p (c n)"),
                                         hat[0:PP, 1, :, :].rearrange("p c n -> p (c n)"), ACT.Copy,
                                         scale=-1.0, bias=1.0).then_inc(ht_s.sem, 1)
                    act.wait_ge(mk_m.sem, mk_m.after(ic + 1))
                    nc.scalar.activation(om[0:PP, 2 * HN:], om[0:PP, 2 * HN:], ACT.Exp).then_inc(mk_e.sem, 1)
                    act.wait_ge(pr_u.sem, pr_u.at(ic))
                    act.wait_ge(oo_p.sem, oo_p.after(ic))
                    nc.scalar.activation(dc, ps[:, 4, 0:T4 * PP], ACT.Copy).then_inc(dc_s.sem, 1)
                    act.wait_ge(oo_p.sem, oo_p.after(ic + 1))
                    act.wait_ge(rs_a.sem, rs_a.at(ic, 0))
                    nc.scalar.activation(res1, ps[:, 5, 0:T4 * PP], ACT.Identity, bias=outb).then_inc(rs_s.sem, 1)
                gn_sqrt(act, i, 1)
                act.wait_ge(gn_ab.sem, gn_ab.at(i, 2))
                act.wait_ge(l2_z.sem, l2_z.at(i))
                nc.scalar.activation(xwb[:, :, 0:1].rearrange("c w s -> c (w s)"), ident[:, 0:NWY], ACT.Identity,
                                     bias=wtok, scale=0.0)
                with act.Fori(0, NWY) as b:
                    ib = i * NWY + b

                    def exps(pr):
                        u = pr % 2
                        act.wait_ge(s_s.sem, s_s.at(ib, pr + 1))
                        act.wait_ge(tr_p.sem, tr_p.at(ib, 4 * (pr - 1) if pr >= 2 else 0))
                        for wi in range(2):
                            ins = nc.scalar.activation(
                                e_sb[u][wi * SLOT:(wi + 1) * SLOT, :, wi * SLOT:wi * SLOT + NTOK],
                                ss[u][wi * SLOT:(wi + 1) * SLOT, :].rearrange("p (o j) -> p o j", o=NH),
                                ACT.Exp, scale=SCALE)
                        ins.then_inc(ex_s.sem, 1)

                    act.wait_ge(v_p.sem, v_p.at(ib, 0))
                    nc.scalar.activation(xwb[:, :, 1:NTOK].rearrange("c w (i j) -> c w i j", i=WS),
                                         x_win[:, bass.ds(b, 1)].rearrange("c a i Y j -> c (a Y) i j"),
                                         ACT.Identity, bias=sm[:, 19:20], scale=sm[:, 18:19]).then_inc(xw_s.sem, 1)
                    for m in range(0, 8, 2):
                        act.wait_ge(qk_p.sem, qk_p.at(ib, m + 1))
                        act.wait_ge(s_p.sem, s_p.at(ib, 0))
                        nc.scalar.activation(qk[:, m, 0:NWY * NTOK], ps[:, 4, 0:NWY * NTOK], ACT.Copy
                                             ).then_inc(qk_a.sem, 1)
                    for pr in range(4):
                        act.wait_ge(v_p.sem, v_p.at(ib, pr + 1))
                        act.wait_ge(pv_p.sem, pv_p.at(ib, 0))
                        nc.scalar.activation(v_sb[pr][:, :, 0:DH],
                                             ps[:, 6 + pr % 2, :].rearrange("p (h d) -> p h d", h=NH), ACT.Copy
                                             ).then_inc(v_s.sem, 1)
                    exps(0)
                    for pr in range(4):
                        u = pr % 2
                        act.wait_ge(pv_p.sem, pv_p.at(ib, pr - 1 if pr >= 2 else 0))
                        for q in (0, 2):
                            act.wait_ge(tr_p.sem, tr_p.at(ib, 4 * pr + q + 1))
                            nc.scalar.activation(et[u][:, q * 512:(q + 1) * 512], ps[:, 4, :], ACT.Copy
                                                 ).then_inc(tr_a.sem, 1)
                        if pr < 3:
                            exps(pr + 1)
                act.wait_ge(tk_v.sem, tk_v.at(i))
                nc.scalar.activation(t8[2], t8[1], ACT.Sqrt, bias=eps_col[:, :], scale=1.0 / DH).then_inc(tk_sd.sem, 1)
                act.wait_ge(tk_s.sem, tk_s.at(i))
                nc.scalar.activation(tok, tok, ACT.Gelu).then_inc(tk_g.sem, 1)
                act.wait_ge(s2_m.sem, s2_m.at(i))
                nc.scalar.activation(s2, s2, ACT.Exp, scale=SCALE).then_inc(s2_e.sem, 1)
                act.wait_ge(a2_p.sem, a2_p.at(i))
                nc.scalar.activation(at2.rearrange("p (a n) -> p a n", a=2), ps[:, 4:6, :], ACT.Copy
                                     ).then_inc(a2_t.sem, 1)
                for nb in range(WS + 1):
                    if nb < WS:
                        act.wait_ge(ag_p.sem, ag_p.at(i, nb + 1))
                        act.wait_ge(y2_p.sem, y2_p.at(i, nb))
                        nc.scalar.activation(ag[:, 0:2, :], ps[:, 0:2, 0:WS * SLOT], ACT.Copy).then_inc(ag_a.sem, 1)
                    if nb:
                        act.wait_ge(y2_p.sem, y2_p.at(i, nb))
                        act.wait_ge(y2_s.sem, y2_s.at(i, nb - 1))
                        nc.scalar.activation(yt, ps[:, 4 + (nb - 1) % 2, 0:WS * SLOT], ACT.Identity, bias=bout
                                             ).then_inc(y2_e.sem, 1)
                gn_sqrt(act, i, 2)
                act.wait_ge(gn_ab.sem, gn_ab.at(i, 3))
                nc.scalar.activation(vp_in, x_yx, ACT.Identity, bias=sm[:, 29:30], scale=sm[:, 28:29]
                                     ).then_inc(v3_s.sem, 1)
                act.wait_ge(mk_s.sem, mk_s.at(i))
                nc.scalar.activation(vp_in, mk, ACT.Relu).then_inc(rl_s.sem, 1)
            own.end()
            ownc.end()

        @block.vector
        def _(dve):
            V = nc.vector
            own = Chain(dve, d_init)
            own.turn(0, 3)
            dve.wait_ge(s_init, INITS)
            dve.wait_ge(s_w, WEIGHTS)
            for tap in range(P9):
                ins = V.tensor_scalar(dwdiag[:, tap, :], ident, dww[:, tap:tap + 1], None, ALU.mult)
            ins.then_inc(s_dw, 1)
            own.step(V.tensor_scalar(keep, filt, 1.0, None, ALU.is_equal))
            own.step(V.tensor_scalar(neg_mw, mw, keep, -1.0, ALU.mult, ALU.mult))
            own.step(V.tensor_scalar(floor2, keep, -2.0, None, ALU.mult))
            own.end()
            own = Chain(dve, d_a)
            with dve.Fori(0, N // 2) as i:
                own.turn(i, DVE_A)
                for u in range(2):
                    n = i * 2 + u
                    g, m = gs[u], gm0[u]
                    dve.wait_ge(a_gram[u].sem, a_gram[u].after(i + 1))
                    own.step(V.tensor_copy(g, ps[:, u, 0:C + 1]))
                    own.step(V.tensor_tensor(junk, g[:, 0:C], ident, ALU.mult))
                    own.step(V.tensor_reduce(st0[u][:, 0:1], junk, AX.X, ALU.add))
                    own.step(V.tensor_copy(st0[u][:, 1:2], g[:, C:C + 1]))
                    V.tensor_scalar(st0[u], st0[u], 1.0 / PIX, None, ALU.mult).then_inc(a_cols.sem, 1)
                    dve.wait_ge(a_gm.sem, a_gm.after(n + 1))
                    own.step(V.tensor_copy(m[:, 0:2], ps[:, 2, 0:2]))
                    own.step(V.scalar_tensor_tensor(m[:, 2:3], m[:, 1:2], m[:, 1:2], m[:, 0:1], ALU.mult, ALU.subtract))
                    V.tensor_scalar(m[:, 2:3], m[:, 2:3], 0.0, None, ALU.min).then_inc(a_var.sem, 1)
                    dve.wait_ge(a_sd.sem, a_sd.after(n + 1))
                    own.step(V.reciprocal(m[:, 4:5], m[:, 3:4]))
                    V.tensor_copy(r0[:, bass.ds(n, 1)], m[:, 4:5])
                    own.step(V.tensor_scalar(u0[:, bass.ds(n, 1)], g[:, C:C + 1], m[:, 4:5], None, ALU.mult))
                    own.step(V.tensor_scalar(q0[:, bass.ds(n, 1)], m[:, 1:2], m[:, 4:5], None, ALU.mult))
                    V.tensor_scalar(gdr[u], ident, m[:, 4:5], None, ALU.mult).then_inc(a_dr.sem, 1)
                    dve.wait_ge(a_scaled.sem, a_scaled.after(n + 1))
                    own.step(V.scalar_tensor_tensor(cacc, ps[:, 3, 0:C], m[:, 4:5], cacc, ALU.mult, ALU.add))
            own.end()
            own = Chain(dve, d_cov)
            own.turn(0, DVE_COV)
            own.step(V.scalar_tensor_tensor(wu0, q0[:, :], float(PIX), u0, ALU.mult, ALU.subtract))
            own.step(V.tensor_reduce(mu0[:, :], wu0, AX.X, ALU.add))
            V.tensor_scalar(mu0[:, :], mu0[:, :], -1.0 / (N * PIX), None, ALU.mult).then_inc(c_d, 1)
            dve.wait_ge(c_p, 1)
            own.step(V.tensor_copy(colT[0:N, :], ps[0:N, 4, 0:3 * C]))
            own.step(V.tensor_scalar(rowT[0:N, 0:C], colT[0:N, C:2 * C], -1.0, None, ALU.mult))
            own.step(V.tensor_copy(junk[0:1, :], ps[0:1, 4, 3 * C:4 * C]))
            V.tensor_scalar(rowT[0:1, C:2 * C], junk[0:1, :], -float(N * PIX), None, ALU.mult).then_inc(c_d, 1)
            dve.wait_ge(c_p, 2)
            own.step(V.tensor_tensor(cacc, cacc, ps[:, 5, 0:C], ALU.add))
            own.step(V.scalar_tensor_tensor(cacc, cacc, 1.0 / (N * PIX), mask16, ALU.mult, ALU.mult))
            own.step(V.scalar_tensor_tensor(aat[:, 0:C], ident, EPS0, cacc, ALU.mult, ALU.add))
            own.step(V.tensor_copy(aat[:, C:], aat[:, 0:C]))
            own.step(V.memset(it[:, 7:8], 3e38))
            own.step(V.memset(it[:, 8:9], -3e38))
            own.step(V.memset(it[:, 9:10], 0.0))
            own.end()
            own = Chain(dve, d_pow)
            with dve.Fori(0, L) as j:
                own.turn(j, DVE_POW)
                n = [0]

                def pe_done():
                    n[0] += 1
                    dve.wait_ge(p_p.sem, p_p.at(j, n[0]))

                own.step(V.tensor_tensor(junk, aat[:, 0:C], ident, ALU.mult))
                V.tensor_reduce(it[:, 0:1], junk, AX.X, ALU.add).then_inc(p_d.sem, 1)
                pe_done()
                own.step(V.tensor_scalar(it[:, 2:3], ps[:, 0, 0:1], 1e-4, 0.25, ALU.max, ALU.mult))
                own.step(V.reciprocal(it[:, 2:3], it[:, 2:3]))
                own.step(V.tensor_copy(it[:, 20:21], vi[:, bass.ds(j, 1)]))
                V.tensor_scalar(bbt, aat, it[:, 2:3], None, ALU.mult).then_inc(p_d.sem, 1)
                pe_done()
                V.tensor_copy(b2, ps[:, 1, 0:2 * C + 1]).then_inc(p_d.sem, 1)
                pe_done()
                V.tensor_copy(b4, ps[:, 2, 0:C + 1]).then_inc(p_d.sem, 1)
                for k in range(3):
                    pe_done()
                    V.tensor_copy(it[:, 1:2], ps[:, 3, k:k + 1]).then_inc(p_d.sem, 1)
                pe_done()
                V.tensor_copy(uw[:, 0:1], ps[:, 3, 3:4]).then_inc(p_d.sem, 1)
                pe_done()
                own.step(V.tensor_copy(uw[:, 1:2], ps[:, 3, 4:5]))
                V.tensor_scalar(uwp, uw, uw[:, 0:1], None, ALU.mult)
                own.step(V.tensor_copy(ubw.rearrange("p (a n) -> p a n", a=2),
                                       uw.rearrange("p (a n) -> p a n", n=1).to_broadcast([C, 2, C])))
                V.tensor_copy(it[:, 21:22], uw[:, 0:1]).then_inc(p_d.sem, 1)
                pe_done()
                own.step(V.tensor_scalar(it[:, 3:5], ps[:, 5, 0:2], 1.0, None, ALU.mult))
                V.tensor_tensor(uwm.rearrange("p (a n) -> p a n", a=2),
                                ps[:, 4, 0:2 * C].rearrange("p (a n) -> p a n", a=2),
                                mask16.rearrange("p (a n) -> p a n", a=1).to_broadcast([C, 2, C]), ALU.mult)
                own.step(V.tensor_scalar(it[:, 5:6], it[:, 3:4], TINY, None, ALU.max))
                own.step(V.reciprocal(it[:, 5:6], it[:, 5:6]))
                own.step(V.tensor_tensor(it[:, 6:7], it[:, 4:5], it[:, 5:6], ALU.mult))
                own.step(V.tensor_tensor(it[:, 13:14], it[:, 7:8], it[:, 6:7], ALU.is_lt))
                own.step(V.tensor_tensor(it[:, 14:15], it[:, 6:7], it[:, 8:9], ALU.is_lt))
                own.step(V.tensor_tensor(it[:, 13:14], it[:, 13:14], it[:, 14:15], ALU.max))
                own.step(V.tensor_tensor(it[:, 9:10], it[:, 9:10], it[:, 13:14], ALU.max))
                own.step(V.tensor_scalar(it[:, 10:11], it[:, 9:10], -1.0, 1.0, ALU.mult, ALU.add))
                own.step(V.tensor_tensor(it[:, 15:16], it[:, 6:7], it[:, 10:11], ALU.mult))
                V.tensor_tensor(it[:, 11:12], it[:, 15:16], it[:, 9:10], ALU.add).then_inc(p_ls.sem, 1)
                own.step(V.scalar_tensor_tensor(it[:, 7:8], it[:, 7:8], it[:, 9:10], it[:, 15:16], ALU.mult, ALU.add))
                V.memset(it[:, 8:9], EPS0)
                own.step(V.tensor_tensor(it[:, 16:17], it[:, 5:6], it[:, 10:11], ALU.mult))
                own.step(V.tensor_scalar(it[:, 17:19], uw, it[:, 16:17], -1.0, ALU.mult, ALU.mult))
                V.scalar_tensor_tensor(aat[:, 0:C], uwm[:, 0:C], it[:, 18:19], aat[:, 0:C], ALU.mult, ALU.add)
                V.scalar_tensor_tensor(aat[:, C:], uwm[:, C:], it[:, 17:18], aat[:, C:], ALU.mult, ALU.add)
                dve.wait_ge(p_sd.sem, p_sd.at(j))
                own.step(V.reciprocal(it[:, 19:20], it[:, 12:13]))
                own.step(V.tensor_scalar(it[:, 19:20], it[:, 19:20], it[:, 17:18], -1.0, ALU.mult, ALU.mult))
                own.step(V.scalar_tensor_tensor(smat, uwm[:, 0:C], it[:, 19:20], smat, ALU.mult, ALU.add))
                assert n[0] == POW_P
            own.end()
            V.tensor_tensor(w0[:, :], smat, w0row, ALU.mult).then_inc(s_w0, 1)
            dve.wait_ge(s_w0, 1)
            own, ownc, ownb, owne = Chain(dve, d_smp), Chain(dve, d_chk), Chain(dve, d_blk), Chain(dve, d_end)

            def group_norm(i, g):
                o = 10 * g
                for k in range(CHUNKS):
                    ins = V.bn_stats(mvs[:, k, :], x[:, k * CH:(k + 1) * CH])
                owne.step(ins)
                alone(dve)
                owne.step(V.bn_aggr(sm[:, o + 1:o + 3], mvs[:, :, :].rearrange("c k s -> c (k s)")))
                V.scalar_tensor_tensor(sm[:, o:o + 1], sm[:, o + 1:o + 2], sm[:, o + 1:o + 2], sm[:, o + 2:o + 3],
                                       ALU.mult, ALU.add).then_inc(gn_st.sem, 1)
                dve.wait_ge(gn_gm.sem, gn_gm.at(i, g + 1))
                owne.step(V.tensor_copy(sm[:, o + 4:o + 6], ps[:, 7, 0:2]))
                owne.step(V.scalar_tensor_tensor(sm[:, o + 3:o + 4], sm[:, o + 5:o + 6], sm[:, o + 5:o + 6],
                                                 sm[:, o + 4:o + 5], ALU.mult, ALU.subtract))
                V.tensor_scalar(sm[:, o + 6:o + 7], sm[:, o + 3:o + 4], 0.0, None, ALU.min).then_inc(gn_var.sem, 1)
                dve.wait_ge(gn_sd.sem, gn_sd.at(i, g + 1))
                owne.step(V.reciprocal(sm[:, o + 8:o + 9], sm[:, o + 7:o + 8]))
                V.tensor_scalar(sm[:, o + 9:o + 10], sm[:, o + 5:o + 6], sm[:, o + 8:o + 9], -1.0, ALU.mult, ALU.mult
                                ).then_inc(gn_ab.sem, 1)

            with dve.Fori(0, N) as i:
                own.turn(i, DVE_SMP)
                owne.turn(i, 15)
                own.step(V.tensor_scalar(w0s[:, :], w0[:, :], r0[:, bass.ds(i, 1)], None, ALU.mult))
                V.tensor_tensor(sm[:, 30:31], q0[:, bass.ds(i, 1)], mu0[:, :], ALU.add).then_inc(l0_w.sem, 1)
                dve.wait_ge(l0_c.sem, l0_c.at(i))
                own.step(V.tensor_tensor(sm[:, 31:32], b0, ps[:, 7, 8:9], ALU.subtract))
                for k in range(CHUNKS):
                    dve.wait_ge(l0_y.sem, l0_y.at(i, k + 1))
                    xk = x[:, k * CH:(k + 1) * CH]
                    ins = V.scalar_tensor_tensor(xk, ps[:, k, 0:CH], sm[:, 31:32], xk, ALU.add, ALU.add)
                own.step(ins)
                group_norm(i, 0)
                dve.wait_ge(z_img.sem, z_img.at(i))
                for k in range(TCH):
                    dve.wait_ge(xp_p.sem, xp_p.at(i, k + 1))
                    V.tensor_tensor(img[0:PP, 2, 2 + k * T4:2 + (k + 1) * T4, :],
                                    ps[0:PP, k, :].rearrange("p (t c) -> p t c", t=T4),
                                    inb_row[:, :].rearrange("p (a c) -> p a c", a=1).to_broadcast([PP, T4, C]),
                                    ALU.add).then_inc(xp_s.sem, 1)
                for k in range(CHUNKS):
                    dve.wait_ge(ln_m.sem, ln_m.at(i, k + 1))
                    yk = y1[:, k * CH:(k + 1) * CH]
                    V.tensor_tensor(yk, yk, ps[:, k, 0:CH], ALU.subtract).then_inc(ln_c.sem, 1)
                for k in range(CHUNKS):
                    yk, sk = y1[:, k * CH:(k + 1) * CH], sd[:, k * CH:(k + 1) * CH]
                    dve.wait_ge(ln_s.sem, ln_s.at(i, k + 1))
                    own.step(V.reciprocal(sk, sk))
                    V.tensor_tensor(yk, yk, sk, ALU.mult).then_inc(ln_y.sem, 1)
                dve.wait_ge(cp_img.sem, cp_img.at(i))
                alone(dve)
                with dve.Fori(0, TCH) as c:
                    ic = i * TCH + c
                    ownc.turn(ic, DVE_CHK)
                    n64 = T4 * G1
                    logits = om[0:PP, 2 * HN:]
                    dve.wait_ge(of_p.sem, of_p.after(ic + 1))
                    dve.wait_ge(ht_s.sem, ht_s.after(ic))
                    for t in range(T4):
                        ins = V.tensor_tensor(om[0:PP, :].rearrange("p (q t g) -> p q t g", t=T4, g=G1)[:, :, t, :],
                                              ps[0:PP, t, 0:OFFS].rearrange("p (q g) -> p q g", g=G1),
                                              offb_row[:, :].rearrange("p (q g) -> p q g", g=G1), ALU.add)
                    ins.then_inc(of_s.sem, 1)
                    dve.wait_ge(of_s.sem, of_s.after(ic + 1))
                    ownc.step(V.tensor_reduce(mx1[0:PP, :], logits.rearrange("p (q n) -> p n q", q=P9), AX.X, ALU.max))
                    by_tap = "p (q n) -> p q n"
                    V.tensor_tensor(logits.rearrange(by_tap, q=P9), logits.rearrange(by_tap, q=P9),
                                    mx1[0:PP, :].rearrange("p (a n) -> p a n", a=1).to_broadcast([PP, P9, n64]),
                                    ALU.subtract).then_inc(mk_m.sem, 1)
                    dve.wait_ge(mk_e.sem, mk_e.after(ic + 1))
                    ownc.step(V.tensor_reduce(sx1[0:PP, :], logits.rearrange("p (q n) -> p n q", q=P9), AX.X, ALU.add))
                    ownc.step(V.reciprocal(sx1[0:PP, :], sx1[0:PP, :]))
                    ownc.step(V.tensor_tensor(logits.rearrange(by_tap, q=P9), logits.rearrange(by_tap, q=P9),
                                              sx1[0:PP, :].rearrange("p (a n) -> p a n", a=1).to_broadcast(
                                                  [PP, P9, n64]), ALU.mult))
                    dve.wait_ge(ht_s.sem, ht_s.after(ic + 1))
                    ownc.step(V.tensor_tensor(hat[0:PP, :, 1, :], hat[0:PP, :, 1, :],
                                              logits.rearrange("p (a n) -> p a n", a=1).to_broadcast([PP, 3, HN]),
                                              ALU.mult))
                    dve.wait_ge(k_z.sem, k_z.after(ic + 1))
                    for k in range(9):
                        aa, bb = k // 3, k % 3
                        t_k = tt[k % 2][0:PP, :]
                        ownc.step(V.tensor_tensor(t_k, hat[0:PP, aa, 1, :], hat[0:PP, bb, 0, :], ALU.mult))
                        k5 = kw[0:PP, :].rearrange("p (y x n) -> p x y n", y=5, x=5)[:, bb:bb + 3, aa:aa + 3, :]
                        ins = V.tensor_tensor(k5, k5, t_k.rearrange("p (x y n) -> p x y n", x=3, y=3), ALU.add)
                        if k < 8:
                            ownc.step(ins)
                    ins.then_inc(k_s.sem, 1)
                    dve.wait_ge(k_s.sem, k_s.after(ic + 1))
                    dve.wait_ge(pr_u.sem, pr_u.at(ic, 0))
                    for s in range(25):
                        if s >= 5:
                            dve.wait_ge(pr_u.sem, pr_u.at(ic, s - 4))
                        taps = kw[0:PP, s * n64:(s + 1) * n64].rearrange("p (n a) -> p n a", a=1)
                        V.tensor_tensor(prod[0:PP, s % 5, :].rearrange("p (n e) -> p n e", e=CG),
                                        taps.to_broadcast([PP, n64, CG]),
                                        img[0:PP, s // 5, bass.ds(c * T4 + s % 5, T4), :].rearrange(
                                            "p x (g e) -> p (x g) e", e=CG), ALU.mult).then_inc(pr_s.sem, 1)
                dve.wait_ge(rs_a.sem, rs_a.at(i * TCH + TCH, 0))
                group_norm(i, 1)
                dve.wait_ge(l2_z.sem, l2_z.at(i))
                alone(dve)
                with dve.Fori(0, NWY) as b:
                    ib = i * NWY + b
                    ownb.turn(ib, 8)

                    def shift(pr):
                        u = pr % 2
                        dve.wait_ge(s_p.sem, s_p.at(ib, pr + 1))
                        sv = ps[:, 0:4, 0:4 * NTOK].rearrange("p r (m j) -> p r m j", m=4)
                        ownb.step(V.tensor_reduce(mxs[u].rearrange("p (r m) -> p r m", r=4), sv, AX.X, ALU.max))
                        dve.wait_ge(ex_s.sem, ex_s.at(ib, pr - 1 if pr >= 2 else 0))
                        V.tensor_tensor(ss[u].rearrange("p (r m j) -> p r m j", r=4, m=4), sv,
                                        mxs[u].rearrange("p (r m a) -> p r m a", r=4, a=1).to_broadcast(
                                            [C, 4, 4, NTOK]), ALU.subtract).then_inc(s_s.sem, 1)

                    for m in range(1, 8, 2):
                        dve.wait_ge(qk_p.sem, qk_p.at(ib, m + 1))
                        dve.wait_ge(s_p.sem, s_p.at(ib, 0))
                        V.tensor_copy(qk[:, m, 0:NWY * NTOK], ps[:, 5, 0:NWY * NTOK]).then_inc(qk_d.sem, 1)
                    shift(0)
                    for pr in range(4):
                        u = pr % 2
                        if pr < 3:
                            shift(pr + 1)
                        dve.wait_ge(pv_p.sem, pv_p.at(ib, pr - 1 if pr >= 2 else 0))
                        for q in (1, 3):
                            dve.wait_ge(tr_p.sem, tr_p.at(ib, 4 * pr + q + 1))
                            V.tensor_copy(et[u][:, q * 512:(q + 1) * 512], ps[:, 5, :]).then_inc(tr_d.sem, 1)
                        dve.wait_ge(pv_p.sem, pv_p.at(ib, pr + 1))
                        pv = ps[:, 6:8, 0:8 * (DH + 1)].rearrange("p a (h d) -> p a h d", h=8)
                        ownb.step(V.reciprocal(rec[u].rearrange("p (a h d) -> p a h d", a=2, d=1), pv[:, :, :, DH:]))
                        dve.wait_ge(wf_in[u].sem, wf_in[u].at(ib, 64 * (pr // 2)))
                        V.tensor_tensor(o_sb[u].rearrange("p (a h d) -> p a h d", a=2, h=8), pv[:, :, :, 0:DH],
                                        rec[u].rearrange("p (a h d) -> p a h d", a=2, d=1).to_broadcast(
                                            [C, 2, 8, DH]), ALU.mult).then_inc(o_s.sem, 1)
                for u in range(2):
                    dve.wait_ge(wf_in[u].sem, wf_in[u].at(i * NWY + NWY, 0))

                def per_head(v):
                    return v.rearrange("p (h d) -> p h d", h=8)

                def spread(v, n):
                    return v.rearrange("p (h a) -> p h a", a=1).to_broadcast([C, 8, n])

                own.step(V.tensor_reduce(t8[0], per_head(wf[:, 0, :]), AX.X, ALU.add))
                own.step(V.tensor_scalar(t8[0], t8[0], 1.0 / DH, None, ALU.mult))
                own.step(V.tensor_tensor(per_head(tok), per_head(wf[:, 0, :]), spread(t8[0], DH), ALU.subtract))
                own.step(V.tensor_tensor(tok2, tok, tok, ALU.mult))
                V.tensor_reduce(t8[1], per_head(tok2), AX.X, ALU.add).then_inc(tk_v.sem, 1)
                dve.wait_ge(tk_sd.sem, tk_sd.at(i))
                own.step(V.reciprocal(t8[3], t8[2]))
                own.step(V.tensor_tensor(per_head(tok), per_head(tok), spread(t8[3], DH), ALU.mult))
                own.step(V.tensor_tensor(per_head(tok), per_head(tok), lnw_row[:, 0:1, :].to_broadcast([C, 8, DH]),
                                         ALU.mult))
                V.tensor_tensor(per_head(tok), per_head(tok), lnw_row[:, 1:2, :].to_broadcast([C, 8, DH]),
                                ALU.add).then_inc(tk_s.sem, 1)
                dve.wait_ge(gt_p.sem, gt_p.at(i))
                V.tensor_copy(gfT.rearrange("p (h k) w -> p k h w", h=2),
                              ps[:, 0, 0:2 * C].rearrange("p (k h w) -> p k h w", k=2, h=2)).then_inc(gt_s.sem, 1)
                dve.wait_ge(q2_p.sem, q2_p.at(i))
                V.tensor_tensor(qk2, ps[:, 1, :].rearrange("p (m w) -> p m w", m=8), spread(bqk, SLOT),
                                ALU.add).then_inc(q2_s.sem, 1)
                dve.wait_ge(s2_p.sem, s2_p.at(i))
                sv = ps[:, 0:4, 0:2 * SLOT].rearrange("p r (k w) -> p r k w", k=2)
                own.step(V.tensor_reduce(t8[4].rearrange("p (r k) -> p r k", r=4), sv, AX.X, ALU.max))
                V.tensor_tensor(s2.rearrange("p (r k w) -> p r k w", r=4, k=2), sv,
                                t8[4].rearrange("p (r k a) -> p r k a", r=4, a=1).to_broadcast([C, 4, 2, SLOT]),
                                ALU.subtract).then_inc(s2_m.sem, 1)
                dve.wait_ge(s2_e.sem, s2_e.at(i))
                own.step(V.tensor_reduce(t8[5], per_head(s2), AX.X, ALU.add))
                own.step(V.reciprocal(t8[5], t8[5]))
                for hh in range(2):
                    rows = slice(hh * SLOT, (hh + 1) * SLOT)
                    ins = V.tensor_tensor(a2[rows, :, rows], per_head(s2)[rows],
                                          t8[5][rows].rearrange("p (h a) -> p h a", a=1).to_broadcast([SLOT, 8, SLOT]),
                                          ALU.mult)
                ins.then_inc(a2_s.sem, 1)
                for nb in range(WS):
                    dve.wait_ge(ag_p.sem, ag_p.at(i, nb + 1))
                    dve.wait_ge(y2_p.sem, y2_p.at(i, nb))
                    V.tensor_copy(ag[:, 2:4, :], ps[:, 2:4, 0:WS * SLOT]).then_inc(ag_d.sem, 1)
                dve.wait_ge(y2_s.sem, y2_s.at(i))
                group_norm(i, 2)
                dve.wait_ge(v3_s.sem, v3_s.at(i))
                V.tensor_reduce(rsum[:, 0:W], vp_in, AX.X, ALU.add)
                own.step(V.tensor_reduce(rsum[:, W:], vp_in.rearrange("c h w -> c w h"), AX.X, ALU.add))
                V.tensor_reduce(sm[:, 34:35], rsum[:, 0:W], AX.X, ALU.add)
                two = "p (a n) -> p a n"
                own.step(V.tensor_tensor(rtmp.rearrange(two, a=2), rsum.rearrange(two, a=2),
                                         idx.rearrange(two, a=1).to_broadcast([C, 2, W]), ALU.mult))
                own.step(V.tensor_reduce(sm[:, 32:34], rtmp.rearrange(two, a=2), AX.X, ALU.add))
                own.step(V.tensor_scalar(sm[:, 34:35], sm[:, 34:35], 1e-9, None, ALU.max))
                own.step(V.reciprocal(sm[:, 34:35], sm[:, 34:35]))
                own.step(V.tensor_scalar(sm[:, 32:34], sm[:, 32:34], sm[:, 34:35], 1.0, ALU.mult, ALU.max))
                own.step(V.tensor_scalar(sm[:, 32:34], sm[:, 32:34], float(H), None, ALU.min))
                own.step(V.tensor_scalar(sm[:, 32:34], sm[:, 32:34], MAGIC, None, ALU.add))
                own.step(V.tensor_scalar(sm[:, 32:34], sm[:, 32:34], MAGIC, None, ALU.subtract))
                own.step(V.tensor_scalar(sm[:, 32:34], sm[:, 32:34], 2.0 / (H - 1), -1.0 - 2.0 / (H - 1), ALU.mult,
                                         ALU.add))
                V.tensor_scalar(axy[:, 0:W], pos, sm[:, 32:33], None, ALU.subtract)
                own.step(V.tensor_scalar(axy[:, W:], pos, sm[:, 33:34], None, ALU.subtract))
                own.step(V.scalar_tensor_tensor(axy, axy, -1.0, axy, ALU.mult, ALU.max))
                own.step(V.tensor_tensor(mk, axy[:, 0:W].rearrange("p (n a) -> p n a", a=1).to_broadcast([C, H, W]),
                                         axy[:, W:].rearrange("p (a n) -> p a n", a=1).to_broadcast([C, H, W]), ALU.add))
                own.step(V.tensor_scalar(mk, mk, neg_mw, floor2, ALU.mult, ALU.max))
                V.scalar_tensor_tensor(mk, mk, 1.0, vp_in, ALU.add, ALU.mult).then_inc(mk_s.sem, 1)
                for k in range(CHUNKS):
                    dve.wait_ge(c3_p.sem, c3_p.at(i, k + 1))
                    xk = x[:, k * CH:(k + 1) * CH]
                    V.scalar_tensor_tensor(xk, ps[:, k, 0:CH], cb, xk, ALU.add, ALU.add).then_inc(c3_s.sem, 1)
            for ch in (own, ownc, ownb, owne):
                ch.end()


def kernel(**inputs):
    import numpy as np
    import concourse.bacc as bacc
    from concourse.bass_utils import run_bass_kernel_spmd

    g = {k: np.asarray(v) for k, v in inputs.items()}
    x = g["x"].reshape(N, C, PIX)
    f = np.float32
    block16 = np.kron(np.eye(GROUPS0), np.ones((L, L)))
    group4 = np.kron(np.eye(C // 4), np.full((4, 4), 0.25))
    off = g["L1_conv_off_w"].reshape(C, G1, P9, 2).transpose(0, 3, 2, 1).reshape(C, 2 * P9 * G1)
    offb = g["L1_conv_off_b"].reshape(G1, P9, 2).transpose(2, 1, 0).reshape(-1)
    msk = g["L1_conv_mask_w"].reshape(C, G1, P9).transpose(0, 2, 1).reshape(C, P9 * G1)
    mskb = g["L1_conv_mask_b"].reshape(G1, P9).T.reshape(-1)
    wqk2 = g["L2_conv_w_qk"].reshape(NH, 2, DH, INNER).transpose(1, 0, 2, 3).reshape(2 * INNER, INNER)
    bqk = g["L2_conv_b_qk"].reshape(NH, 2, DH).transpose(1, 0, 2).reshape(8, C).T
    col = [g["L0_conv_bias"].reshape(C), g["L1_conv_dw_b"], g["L1_conv_ln_g"], g["L1_conv_ln_b"], g["L1_conv_out_b"],
           g["L2_conv_b_out"], g["L3_conv_bias"], g["L3_conv_mask_weight"], g["L3_conv_filter"].reshape(C),
           g["L2_conv_window_tokens"]]
    arrays = {
        "x": x,
        "x_t": x.transpose(0, 2, 1),
        "c_mats": np.stack([np.eye(C), block16, group4, np.full((C, C), 1.0 / C)], 1).astype(f),
        "c_pos": np.broadcast_to(np.stack([np.linspace(-1, 1, H), np.arange(1, H + 1)])[None], (C, 2, W)).astype(f),
        "cols": np.concatenate([np.stack(col, 1), g["L1_conv_dw_w"].reshape(C, 9), bqk], 1),
        "v_init": g["L0_conv_v_init"].transpose(0, 2, 1).reshape(C, L),
        "w0_row": g["L0_conv_weight"].reshape(C),
        "in_w": g["L1_conv_in_w"], "out_w": g["L1_conv_out_w"],
        "offm_w": np.concatenate([off, msk], 1), "offm_b": np.concatenate([offb, mskb]),
        "in_b": g["L1_conv_in_b"],
        "wqk": g["L2_conv_w_qkv"][:2 * INNER].T, "wv": g["L2_conv_w_qkv"][2 * INNER:].T,
        "wqk2": wqk2.T.reshape(4, C, 2 * INNER).transpose(1, 0, 2),
        "wout": g["L2_conv_w_out"].T.reshape(4, C, C).transpose(1, 0, 2),
        "convw": g["L3_conv_weight"].reshape(C, C, 9).transpose(1, 2, 0),
        "ln2_w": g["L2_conv_ln_w"], "ln2_b": g["L2_conv_ln_b"],
    }
    nc = bacc.Bacc("TRN2", target_bir_lowering=False, num_devices=1)
    feed, aps = {}, {}
    for name, v in arrays.items():
        feed[f"in_{name}"] = np.ascontiguousarray(v)
        aps[name] = nc.dram_tensor(f"in_{name}", v.shape, F32, kind="ExternalInput").ap()
    aps["out"] = nc.dram_tensor("out_x", (N, C, PIX), F32, kind="ExternalOutput").ap()
    build(nc, aps)
    r = run_bass_kernel_spmd(nc, [feed], core_ids=[0])
    return r.results[0]["out_x"].reshape(N, C, H, W)
```

```python
from contextlib import ExitStack

import concourse.bass as bass
from concourse import mybir

F32 = mybir.dt.float32
I32 = mybir.dt.int32
ALU = mybir.AluOpType
ACT = mybir.ActivationFunctionType
AX = mybir.AxisListType

N, C, H, W = 16, 128, 56, 56
PIX = H * W
GN_EPS = 1e-5
LN_EPS = 1e-5
EPS0 = 1e-4
GROUPS0 = 8
L = C // GROUPS0
G1, P9, CG = 16, 9, 8
ROWS = 8
CHUNKS = H // ROWS
CH = ROWS * W
HALF = W // 2
PP = 2 * H
TILES = HALF
T4 = 4
TCH = TILES // T4
NH, DH, WS = 16, 32, 7
NWY = W // WS
NTOK = WS * WS + 1
SLOT = 64
INNER = NH * DH
VD = DH + 1
SCALE = float(DH) ** -0.5
SHIFTS = 5
TAPS = SHIFTS * SHIFTS
PRODS = 5
IMGX = HALF + 4
OFFS = 3 * P9 * G1
POW_D, POW_P = 9, 9
ACT_SMP, ACT_CHK = 1, 1
DVE_A, DVE_COV, DVE_POW, DVE_SMP, DVE_CHK = 20, 12, 22, 50, 23
DW_PE = 6
PREPARE_AT, STEPS_AT = 3, 8
PROJECT_AT = 12
MAGIC = 12582912.0
TINY = 1e-37

PRIME = 1


class Signal:

    def __init__(self, sem, per, prime):
        self.sem, self.per, self.prime = sem, per, prime

    def after(self, n):
        return n + self.prime

    def at(self, i, k=None):
        return i * self.per + (self.per if k is None else k) + self.prime


class Chain:

    def __init__(self, eng, sem):
        self.eng, self.sem, self.base, self.n = eng, sem, 0, 0

    def turn(self, i, per):
        if self.n:
            self.end()
        self.base, self.n, self.per = i * per, 0, per

    def end(self):
        assert self.per == self.n, (self.sem, self.per, self.n)

    def step(self, ins):
        self.mark(ins)
        self.settle()

    def mark(self, ins):
        ins.then_inc(self.sem, 1)
        self.n += 1

    def settle(self):
        self.eng.wait_ge(self.sem, self.base + self.n)


def build(nc, a):
    with ExitStack() as ctx:
        def sb(name, shape, dt=F32):
            return ctx.enter_context(nc.sbuf_tensor(name, shape, dt))

        def sem(name):
            return ctx.enter_context(nc.semaphore(name))

        cst = sb("cst", [C, 4, C])
        ident, mask16, gavg, mean128 = (cst[:, k, :] for k in range(4))
        posidx = sb("posidx", [C, 2, W])
        pos, idx = posidx[:, 0, :], posidx[:, 1, :]
        inw = sb("inw", [C, C])
        outw = sb("outw", [C, C])
        offw = sb("offw", [C, OFFS])
        dwdiag = sb("dwdiag", [C, P9, C])
        wqk = sb("wqk", [C, 2 * INNER])
        wv = sb("wv", [C, INNER])
        wqk2 = sb("wqk2", [C, 4, 2 * INNER])
        wqk2_room = wqk2[:, :, :].rearrange("p k n -> p (k n)")
        wout = sb("wout", [C, 4, C])
        convw = sb("convw", [C, 9, C])
        inb_row = sb("inb_row", [PP, C])
        offb_row = sb("offb_row", [PP, OFFS])
        lnw_row = sb("lnw_row", [C, 2, DH])
        cols = sb("cols", [C, 32])
        b0, dwb, lng, lnb, outb, bout, cb, mw, filt, wtok = (cols[:, k:k + 1] for k in range(10))
        dww = cols[:, 10:19]
        bqk = cols[:, 19:27]
        keep = cols[:, 27:28]
        neg_mw = cols[:, 28:29]
        floor2 = cols[:, 29:30]
        w0 = sb("w0", [C, C])
        w0s = sb("w0s", [C, C])
        r0 = sb("r0", [C, N])
        q0 = sb("q0", [C, N])
        mu0 = sb("mu0", [C, 1])
        eps_col = sb("eps_col", [C, 1])
        mvs = sb("mvs", [C, CHUNKS, 6])
        sm = sb("sm", [C, 48])
        near = sb("near", [C, 4])
        far = sb("far", [1, 1], I32)
        x = sb("x", [C, PIX])
        vp = sb("vp", [C, H + 2, W + 2])
        x_yx = x[:, :].rearrange("c (h w) -> c h w", h=H)
        x_tile = x[:, :].rearrange("c (p k t) -> c k t p", k=TCH, t=T4)
        x_win = x[:, :].rearrange("c (X i Y j) -> c X i Y j", X=NWY, i=WS, Y=NWY, j=WS)
        vp_in = vp[:, 1:H + 1, 1:W + 1]
        IMG = SHIFTS * IMGX * C
        HN = P9 * T4 * G1
        HATS_AT = IMG + PIX + T4 * PP + 3 * HN
        ARENA = HATS_AT + 6 * HN + 2 * HN + 2 * TAPS * T4 * G1 + T4 * C + 2 * T4 * PP + 2 * T4 * G1
        arena = sb("arena", [C, ARENA])

        def carver(start=0):
            at = [start]

            def carve(n):
                v = arena[:, at[0]:at[0] + n]
                at[0] += n
                assert at[0] <= ARENA, at[0]
                return v
            return carve

        cv = carver()
        xt = [cv(TILES * (C + 1)).rearrange("p (t c) -> p t c", t=TILES) for _ in range(2)]
        gs = [cv(C + 1) for _ in range(2)]
        gdr = [cv(C) for _ in range(2)]
        cacc, junk = cv(C), cv(C)
        st0 = [cv(2) for _ in range(2)]
        gm0 = [cv(6) for _ in range(2)]
        u0, wu0 = cv(N), cv(N)
        colT, rowT = cv(3 * C), cv(2 * C)
        aat, bbt, b2, b4 = cv(2 * C), cv(2 * C), cv(2 * C + 1), cv(C + 1)
        vi = cv(L)
        uw, uwp = cv(2), cv(2)
        ubw, uwm = cv(2 * C), cv(2 * C)
        smat, w0row = cv(C), cv(C)
        it = cv(24)
        cv = carver()
        img = cv(IMG).rearrange("p (a x c) -> p a x c", a=SHIFTS, x=IMGX)
        y1 = cv(PIX)
        gc = cv(T4 * PP)
        om = cv(3 * HN)
        hat = cv(6 * HN).rearrange("p (a c n) -> p a c n", a=3, c=2)
        tt = [cv(HN) for _ in range(2)]
        kw = [cv(TAPS * T4 * G1) for _ in range(2)]
        prod = wqk2_room[:, 0:PRODS * T4 * C].rearrange("p (k n) -> p k n", k=PRODS)
        total = cv(T4 * C)
        dc = cv(T4 * PP)
        res1 = cv(T4 * PP)
        mx1 = cv(T4 * G1)
        sx1 = cv(T4 * G1)
        cv = carver(HATS_AT)
        sq = [cv(CH) for _ in range(2)]
        sd = cv(PIX)
        y1_tile = y1.rearrange("c (p k t) -> c k t p", k=TCH, t=T4)
        cv = carver(HATS_AT)
        my, dist, acc, part, at0 = cv(HN), cv(HN), cv(T4 * C), cv(T4 * C), cv(2 * P9 * T4)
        src_y, src_x, first_x = cv(1), cv(1), cv(1)
        row = wqk2_room[:, 0:HALF * C].rearrange("p (x c) -> p x c", c=C)
        cv = carver()
        QW = NWY * NTOK + SLOT - NTOK
        xwb = cv(NWY * SLOT).rearrange("p (w s) -> p w s", w=NWY)
        qk = cv(8 * QW).rearrange("p (m n) -> p m n", m=8)
        v_sb = [cv(NH * VD * 2).rearrange("p (k d) -> p k d", k=NH) for _ in range(4)]
        ss = [cv(NH * NTOK) for _ in range(2)]
        e_sb = [cv(NH * SLOT).rearrange("p (o j) -> p o j", o=NH) for _ in range(2)]
        et = [cv(NH * SLOT) for _ in range(2)]
        o_sb = [cv(INNER) for _ in range(2)]
        wf = cv(NTOK * INNER // 2).rearrange("p (n c) -> p n c", n=NTOK)
        at2 = cv(8 * C)
        a2 = cv(8 * C).rearrange("p (h w) -> p h w", h=8)
        ag = cv(4 * WS * SLOT).rearrange("p (m n) -> p m n", m=4)
        yt = cv(WS * SLOT)
        mxs = [cv(NH) for _ in range(2)]
        rec = [cv(NH) for _ in range(2)]
        cv = carver(NWY * SLOT)
        tok, tok2 = cv(8 * DH), cv(8 * DH)
        gfT = cv(4 * SLOT).rearrange("p (m w) -> p m w", m=4)
        qk2 = cv(8 * SLOT).rearrange("p (m w) -> p m w", m=8)
        s2 = cv(8 * SLOT)
        t8 = [cv(8) for _ in range(6)]
        cv = carver(HATS_AT)
        mk = cv(PIX).rearrange("p (h w) -> p h w", h=H)
        axy, rsum, rtmp = cv(2 * W), cv(2 * W), cv(2 * W)

        ps = ctx.enter_context(nc.psum_tensor("ps", [C, 8, 512], F32))

        signals = []

        def sig(name, per=1, prime=PRIME):
            signals.append(Signal(sem(name), per, prime))
            return signals[-1]

        s_w = sem("weights_loaded")
        s_init = sem("init_done")
        s_passed = sem("waits_passed")
        s_dw = sem("dwdiag_built")
        d_init, d_a, d_cov, d_pow, d_smp, d_chk, d_blk, d_end, d_prep = (sem(f"dve_own_{k}") for k in range(9))
        t_smp, t_chk = sem("act_own_sample"), sem("act_own_chunk")
        a_xt = [sig("a_xt0", 16), sig("a_xt1", 16)]
        a_gram = [sig("a_gram0"), sig("a_gram1")]
        a_cols, a_gm, a_var, a_sd = sig("a_cols"), sig("a_gm"), sig("a_var"), sig("a_sd")
        a_dr, a_scaled = sig("a_dr"), sig("a_scaled")
        c_d, c_p = sem("cov_dve"), sem("cov_pe")
        p_d, p_p = sig("pow_dve", POW_D), sig("pow_pe", POW_P)
        p_ls, p_sd = sig("pow_lambda"), sig("pow_sqrt")
        s_w0 = sem("w0_ready")
        x_in, x_out = sig("x_in", 16), sig("x_out", 16 * CHUNKS)
        l0_w, l0_c, l0_y = sig("l0_weights"), sig("l0_const"), sig("l0_psum", CHUNKS)
        gn_st, gn_gm, gn_var, gn_sd, gn_ab = (sig(f"gn_{k}", 3) for k in ("stats", "group", "var", "sd", "ab"))
        v1_in = sig("v1_in")
        xp_p, xp_s = sig("xproj_psum", TCH), sig("xproj_sbuf", TCH)
        z_img = sig("images_zeroed")
        cp_img = sig("images_shifted", 14 * 16)
        dw_p, dw_s, dw_f = sig("dw_psum", CHUNKS), sig("dw_sbuf", CHUNKS), sig("dw_full", CHUNKS)
        ln_m, ln_c, ln_q, ln_v, ln_s, ln_y = (sig(f"ln_{k}", CHUNKS) for k in
                                              ("mean", "centred", "square", "var", "sd", "normed"))
        gc_s, of_p, of_s, mk_m, mk_e, ht_s = (sig(k) for k in ("gelu_chunk", "off_psum", "off_sbuf", "mask_shifted",
                                                               "mask_exp", "hats"))
        k_z, k_s = sig("taps_zeroed", TCH + 1), sig("taps_built")
        pr_s, pr_u = sig("prod_ready", TAPS), sig("prod_used", TAPS, PRODS)
        sum_s, sum_t = sig("sum_sbuf"), sig("sum_turned")
        dc_s, oo_p, rs_s, rs_a = sig("dc_sbuf"), sig("out1_psum"), sig("res1_sbuf"), sig("res1_added")
        nf_d, nf_p, nf_s, l1_s = sig("near_sbuf"), sig("near_psum"), sig("far_sbuf"), sig("l1_done")
        f_go, f_x, f_t, f_l, f_row, f_used, f_d, f_a, f_p, f_o, f_oy, f_ox = f_all = [
            sem(f"far_{k}") for k in ("go", "x", "image", "l0", "row", "row_used", "dve", "act", "pe", "own", "own_row",
                                      "own_pixel")]
        wq_in, v_one = sig("wqk2_loaded", 16), sig("v_ones")
        l2_z, xw_s = sig("l2_zeroed", 6), sig("xwin")
        qk_p, qk_a, qk_d = sig("qk_psum", 8), sig("qk_sbuf_act", 4), sig("qk_sbuf_dve", 4)
        s_p, s_s, v_p, v_s, ex_s = sig("s_psum", 4), sig("s_shifted", 4), sig("v_psum", 4), sig("v_sbuf", 4), sig("exps", 4)
        tr_p, tr_a, tr_d = sig("et_psum", 8), sig("et_sbuf_act", 4), sig("et_sbuf_dve", 4)
        pv_p, o_s = sig("pv_psum", 4), sig("o_sbuf", 4)
        wf_in = [sig("wf_in0", 2 * 64), sig("wf_in1", 2 * 64)]
        (tk_v, tk_sd, tk_s, tk_g, gt_p, gt_s, q2_p, q2_s, s2_p, s2_m, s2_e, a2_s, a2_p, a2_t) = (
            sig(k) for k in ("tok_var", "tok_sd", "tok_normed", "tok_gelu", "gft_psum", "gft_sbuf", "qk2_psum",
                             "qk2_sbuf", "s2_psum", "s2_shifted", "s2_exp", "a2_sbuf", "a2t_psum", "a2t_sbuf"))
        ag_p, ag_a, ag_d = sig("agg_psum", WS), sig("agg_act", WS), sig("agg_dve", WS)
        y2_p, y2_e, y2_s = sig("y2_psum", WS), sig("y2_sbuf", WS), sig("y2_added", WS)
        v3_s, mk_s, rl_s = sig("v3"), sig("masked"), sig("relu")
        c3_p, c3_s = sig("conv_psum", CHUNKS), sig("conv_added", CHUNKS)

        block = ctx.enter_context(nc.Block())
        WEIGHTS = 16 * 16
        INITS = 6

        def alone(eng):
            eng.sem_inc(s_passed, 1)

        def is_far(eng, i):
            eng.wait_ge(nf_s.sem, nf_s.at(i))
            alone(eng)
            return eng.value_load(far[0:1, 0:1], min_val=0, max_val=1) != 0

        def heads():
            return [(r * 4 + m, 4 * m + r, m, r) for m in range(4) for r in range(4)]

        def heads2():
            return [(r * 2 + kk, hh, kk, r) for hh in range(2) for kk in range(2) for r in range(4)]

        @block.sync
        def _(sp):
            loads = [(cst[:, :, :], a["c_mats"]), (posidx[:, :, :], a["c_pos"]), (cols[:, 0:27], a["cols"]),
                     (vi, a["v_init"]), (w0row, a["w0_row"].partition_broadcast(C)),
                     (inw[:, :], a["in_w"]), (outw[:, :], a["out_w"]), (offw[:, :], a["offm_w"]),
                     (wqk[:, :], a["wqk"]), (wv[:, :], a["wv"]),
                     (wout[:, :, :], a["wout"]), (convw[:, :, :], a["convw"]),
                     (inb_row[:, :], a["in_b"].partition_broadcast(PP)),
                     (offb_row[:, :], a["offm_b"].partition_broadcast(PP)),
                     (lnw_row[:, 0, :], a["ln2_w"].partition_broadcast(C)),
                     (lnw_row[:, 1, :], a["ln2_b"].partition_broadcast(C))]
            for dst, src in loads:
                sp.dma_start(dst, src).then_inc(s_w, 16)
            with sp.Fori(0, N // 2) as i:
                for u in range(2):
                    sp.wait_ge(a_gram[u].sem, a_gram[u].after(i))
                    sp.dma_start(xt[u][0:PP, :, 0:C], a["x_t"][bass.ds(i * 2 + u, 1)].rearrange(
                        "a (p t) c -> p (a t) c", t=TILES)).then_inc(a_xt[u].sem, 16)
            sp.wait_ge(s_w0, 1)
            with sp.Fori(0, N) as i:
                sp.wait_ge(y2_s.sem, y2_s.at(i, 0))
                sp.dma_start(y1, a["x"][bass.ds(i, 1)].rearrange("a c n -> c (a n)")).then_inc(x_in.sem, 16)
                sp.wait_ge(xp_s.sem, xp_s.at(i))
                for s in (2, 0, 1, 3, 4):
                    d = s - 2
                    lo, hi = max(0, -d), H - max(0, d)
                    if d:
                        sp.dma_start(img[2 * lo:2 * hi, s, 2:2 + HALF, :],
                                     img[2 * (lo + d):2 * (hi + d), 2, 2:2 + HALF, :]).then_inc(cp_img.sem, 16)
                    sp.dma_start(img[2 * lo:2 * hi:2, s, 2 + HALF:, :],
                                 img[2 * (lo + d) + 1:2 * (hi + d):2, 2, 2:4, :]).then_inc(cp_img.sem, 16)
                    sp.dma_start(img[2 * lo + 1:2 * hi:2, s, 0:2, :],
                                 img[2 * (lo + d):2 * (hi + d):2, 2, HALF:HALF + 2, :]).then_inc(cp_img.sem, 16)
                with sp.If(is_far(sp, i)):
                    sp.wait_ge(f_go, 1)
                    sp.dma_start(x[:, :], a["x"][bass.ds(i, 1)].rearrange("a c n -> c (a n)")).then_inc(f_x, 16)
                    sp.dma_start(a["img_rows"], img[0:PP, 2, 2:2 + HALF, :]).then_inc(f_t, 16)
                    sp.dma_start(at0[0:PP, :], a["c_places"]).then_inc(f_t, 16)
                    sp.wait_ge(f_t, 32)
                    with sp.Fori(0, TCH) as c:
                        with sp.Fori(0, PP) as p:
                            sp.wait_ge(f_used, c * PP + p + 1)
                            sp.dma_start(row[0:PP, :, :], a["img_rows"][bass.ds(p, 1)].rearrange(
                                "a x c -> (a x) c").partition_broadcast(PP)).then_inc(f_row, 16)
                sp.wait_ge(l1_s.sem, l1_s.at(i))
                sp.dma_start(wqk2[:, :, :], a["wqk2"]).then_inc(wq_in.sem, 16)
                for b in range(NWY):
                    for pr in range(4):
                        sp.wait_ge(o_s.sem, o_s.after(i * NWY * 4 + b * 4 + pr + 1))
                        for wi in range(2):
                            for hh in range(2):
                                w = b * NWY + 2 * pr + wi
                                sp.dma_start(wf[hh * SLOT + w:hh * SLOT + w + 1, :, :],
                                             o_sb[pr % 2][wi * SLOT:wi * SLOT + NTOK, hh * 256:(hh + 1) * 256]
                                             ).then_inc(wf_in[pr % 2].sem, 16)
            sp.wait_ge(x_out.sem, x_out.at(N, 0))

        @block.gpsimd
        def _(pool):
            for sg in signals:
                pool.sem_inc(sg.sem, sg.prime)
            for u in range(2):
                nc.gpsimd.memset(xt[u][0:PP, :, C:C + 1], 1.0).then_inc(s_init, 1)
            nc.gpsimd.memset(cacc, 0.0).then_inc(s_init, 1)
            nc.gpsimd.memset(smat, 0.0).then_inc(s_init, 1)
            nc.gpsimd.memset(vp[:, :, :], 0.0).then_inc(s_init, 1)
            nc.gpsimd.memset(eps_col[:, :], GN_EPS).then_inc(s_init, 1)
            pool.wait_ge(s_w0, 1)
            with pool.Fori(0, N) as i:
                pool.wait_ge(y2_s.sem, y2_s.at(i, 0))
                alone(pool)
                nc.gpsimd.memset(img[0:PP, :, :, :].rearrange("p a x c -> p (a x c)"), 0.0).then_inc(z_img.sem, 1)
                pool.wait_ge(c3_s.sem, c3_s.at(i, 0))
                alone(pool)
                pool.wait_ge(ln_y.sem, ln_y.at(i))
                alone(pool)
                for u in range(2):
                    nc.gpsimd.memset(kw[u][0:PP, :], 0.0).then_inc(k_z.sem, 1)

                def add_chunk(ic, c):
                    xv = x_tile[:, c, :, :].rearrange("c k t p -> c (k t) p")
                    pool.wait_ge(rs_s.sem, rs_s.after(ic + 1))
                    nc.gpsimd.tensor_tensor(xv, xv, res1.rearrange("c (t p) -> c t p", t=T4), ALU.add
                                            ).then_inc(rs_a.sem, 1)

                with pool.Fori(0, TCH // 2) as j:
                    for u in range(2):
                        ic = i * TCH + j * 2 + u
                        pool.wait_ge(pr_s.sem, pr_s.after((ic + 1) * TAPS))
                        alone(pool)
                        nc.gpsimd.memset(kw[u][0:PP, :], 0.0).then_inc(k_z.sem, 1)
                        add_chunk(ic, bass.ds(j * 2 + u, 1))
                add_chunk(i * TCH + TCH - 1, slice(TCH - 1, TCH))
                pool.wait_ge(rs_a.sem, rs_a.at(i * TCH + TCH, 0))
                pool.wait_ge(l1_s.sem, l1_s.at(i))
                alone(pool)
                nc.gpsimd.memset(xwb, 0.0).then_inc(l2_z.sem, 1)
                nc.gpsimd.memset(qk[:, :, NWY * NTOK:], 0.0).then_inc(l2_z.sem, 1)
                for u in range(2):
                    nc.gpsimd.memset(e_sb[u][:, :, NTOK:], 0.0).then_inc(l2_z.sem, 1)
                for u in range(4):
                    ins = nc.gpsimd.memset(v_sb[u], 0.0)
                ins.then_inc(l2_z.sem, 1)
                nc.gpsimd.memset(a2, 0.0).then_inc(l2_z.sem, 1)
                for nb in range(WS):
                    pool.wait_ge(y2_e.sem, y2_e.at(i, nb + 1))
                    alone(pool)
                    xv = x_win[:, :, nb, :, :]
                    yv = yt.rearrange("c (j X Y) -> c X Y j", j=WS, X=NWY)
                    nc.gpsimd.tensor_tensor(xv, xv, yv, ALU.add).then_inc(y2_s.sem, 1)

        def gn_group(pe, i, g):
            o = 10 * g
            pe.wait_ge(gn_st.sem, gn_st.at(i, g + 1))
            nc.tensor.matmul(ps[:, 7, 0:2], gavg, sm[:, o:o + 2], start=True, stop=True).then_inc(gn_gm.sem, 1)

        def conv3(pe, k, weights, taps, done):
            for tap in range(taps):
                dy, dx = tap // 3, tap % 3
                mm = nc.tensor.matmul(ps[:, k, 0:CH], weights[:, tap, :],
                                      vp[:, ROWS * k + dy:ROWS * k + dy + ROWS, dx:dx + W],
                                      start=(tap == 0), stop=(tap == taps - 1))
            mm.then_inc(done.sem, 1)

        @block.tensor
        def _(pe):
            pe.wait_ge(s_init, INITS)
            pe.wait_ge(s_w, WEIGHTS)
            with pe.Fori(0, N // 2) as i:
                for u in range(2):
                    pe.wait_ge(a_xt[u].sem, a_xt[u].at(i))
                    pe.wait_ge(a_dr.sem, a_dr.after(i * 2))
                    for t in range(TILES):
                        mm = nc.tensor.matmul(ps[:, u, 0:C + 1], xt[u][0:PP, t, 0:C], xt[u][0:PP, t, :],
                                              start=(t == 0), stop=(t == TILES - 1))
                    mm.then_inc(a_gram[u].sem, 1)
                for u in range(2):
                    pe.wait_ge(a_cols.sem, a_cols.after(i * 2 + u + 1))
                    nc.tensor.matmul(ps[:, 2, 0:2], gavg, st0[u], start=True, stop=True).then_inc(a_gm.sem, 1)
                    pe.wait_ge(a_dr.sem, a_dr.after(i * 2 + u + 1))
                    nc.tensor.matmul(ps[:, 3, 0:C], gs[u][:, 0:C], gdr[u], start=True, stop=True
                                     ).then_inc(a_scaled.sem, 1)
            pe.wait_ge(c_d, 1)
            for k, v in enumerate((u0, q0[:, :], wu0)):
                nc.tensor.transpose(ps[0:N, 4, k * C:(k + 1) * C], v, ident)
            nc.tensor.transpose(ps[0:1, 4, 3 * C:4 * C], mu0[:, :], ident).then_inc(c_p, 1)
            pe.wait_ge(c_d, 2)
            nc.tensor.matmul(ps[:, 5, 0:C], colT[0:N, 0:C], rowT[0:N, 0:C], start=True, stop=False)
            nc.tensor.matmul(ps[:, 5, 0:C], colT[0:N, C:2 * C], colT[0:N, 2 * C:3 * C], start=False, stop=False)
            nc.tensor.matmul(ps[:, 5, 0:C], junk[0:1, :], rowT[0:1, C:2 * C], start=False, stop=True).then_inc(c_p, 1)
            with pe.Fori(0, L) as j:
                n = [0]

                def after(k=1):
                    n[0] += k
                    pe.wait_ge(p_d.sem, p_d.at(j, n[0]))

                after()
                nc.tensor.matmul(ps[:, 0, 0:1], mask16, it[:, 0:1], start=True, stop=True).then_inc(p_p.sem, 1)
                after()
                nc.tensor.matmul(ps[:, 1, 0:C], bbt[:, C:], bbt[:, 0:C], start=True, stop=True)
                nc.tensor.matmul(ps[:, 1, C:2 * C], bbt[:, 0:C], bbt[:, C:], start=True, stop=True)
                nc.tensor.matmul(ps[:, 1, 2 * C:2 * C + 1], bbt[:, C:], it[:, 20:21], start=True, stop=True
                                 ).then_inc(p_p.sem, 1)
                after()
                nc.tensor.matmul(ps[:, 2, 0:C], b2[:, 0:C], b2[:, C:2 * C], start=True, stop=True)
                nc.tensor.matmul(ps[:, 2, C:C + 1], b2[:, C:2 * C], b2[:, 2 * C:], start=True, stop=True
                                 ).then_inc(p_p.sem, 1)
                after()
                for k in range(4):
                    if k:
                        after()
                    nc.tensor.matmul(ps[:, 3, k:k + 1], b4[:, 0:C], b4[:, C:] if k == 0 else it[:, 1:2],
                                     start=True, stop=True).then_inc(p_p.sem, 1)
                after()
                nc.tensor.matmul(ps[:, 3, 4:5], aat[:, C:], uw[:, 0:1], start=True, stop=True).then_inc(p_p.sem, 1)
                after()
                nc.tensor.matmul(ps[:, 4, 0:C], ubw[:, 0:C], ident, start=True, stop=True)
                nc.tensor.matmul(ps[:, 4, C:2 * C], ubw[:, C:], ident, start=True, stop=True)
                nc.tensor.matmul(ps[:, 5, 0:2], mask16, uwp, start=True, stop=True).then_inc(p_p.sem, 1)
                assert n[0] == POW_D
            with pe.Fori(0, N) as i:
                pe.wait_ge(l0_w.sem, l0_w.at(i))
                pe.wait_ge(x_in.sem, x_in.at(i))
                pe.wait_ge(c3_s.sem, c3_s.at(i, 0))
                nc.tensor.matmul(ps[:, 7, 8:9], w0[:, :], sm[:, 30:31], start=True, stop=True).then_inc(l0_c.sem, 1)
                for k in range(CHUNKS):
                    nc.tensor.matmul(ps[:, k, 0:CH], w0s[:, :], y1[:, k * CH:(k + 1) * CH], start=True, stop=True
                                     ).then_inc(l0_y.sem, 1)
                gn_group(pe, i, 0)
                pe.wait_ge(v1_in.sem, v1_in.at(i))
                for k in range(TCH):
                    for t in range(T4):
                        mm = nc.tensor.matmul(ps[0:PP, k, t * C:(t + 1) * C],
                                              sd.rearrange("c (p x) -> c x p", x=HALF)[:, k * T4 + t, :], inw[:, :],
                                              start=True, stop=True)
                    mm.then_inc(xp_p.sem, 1)
                for t in range(CHUNKS + 2):
                    if t < CHUNKS:
                        pe.wait_ge(xp_s.sem, xp_s.at(i, t + 1))
                        conv3(pe, t, dwdiag, DW_PE, dw_p)
                    k = t - 1
                    if 0 <= k < CHUNKS:
                        pe.wait_ge(dw_f.sem, dw_f.at(i, k + 1))
                        nc.tensor.matmul(ps[:, k, 0:CH], mean128, y1[:, k * CH:(k + 1) * CH], start=True, stop=True
                                         ).then_inc(ln_m.sem, 1)
                    k = t - 2
                    if 0 <= k < CHUNKS:
                        pe.wait_ge(ln_q.sem, ln_q.at(i, k + 1))
                        nc.tensor.matmul(ps[:, k, 0:CH], mean128, sq[k % 2], start=True, stop=True
                                         ).then_inc(ln_v.sem, 1)
                pe.wait_ge(ln_s.sem, ln_s.at(i))

                def project(ic):
                    pe.wait_ge(gc_s.sem, gc_s.after(ic + 1))
                    pe.wait_ge(of_s.sem, of_s.after(ic))
                    for t in range(T4):
                        mm = nc.tensor.matmul(ps[0:PP, t, 0:OFFS], gc[:, t * PP:(t + 1) * PP], offw[:, :],
                                              start=True, stop=True)
                    mm.then_inc(of_p.sem, 1)

                def collect(ic, ahead):
                    pe.wait_ge(sum_s.sem, sum_s.after(ic))
                    for s in range(TAPS):
                        if s == PROJECT_AT and ahead:
                            project(ic + 2)
                        pe.wait_ge(pr_s.sem, pr_s.after(ic * TAPS + s + 1))
                        nc.tensor.matmul(ps[0:PP, 4, :], ident[0:PP, 0:PP], prod[0:PP, s % PRODS, :],
                                         start=(s == 0), stop=(s == TAPS - 1)).then_inc(pr_u.sem, 1)
                    pe.wait_ge(sum_s.sem, sum_s.after(ic + 1))
                    pe.wait_ge(dc_s.sem, dc_s.after(ic))
                    for t in range(T4):
                        mm = nc.tensor.transpose(ps[:, 6, t * PP:(t + 1) * PP], total[0:PP, t * C:(t + 1) * C],
                                                 ident[0:PP, 0:PP])
                    mm.then_inc(sum_t.sem, 1)
                    pe.wait_ge(dc_s.sem, dc_s.after(ic + 1))
                    pe.wait_ge(rs_s.sem, rs_s.after(ic))
                    nc.tensor.matmul(ps[:, 5, 0:T4 * PP], outw[:, :], dc, start=True, stop=True).then_inc(oo_p.sem, 1)

                project(i * TCH)
                project(i * TCH + 1)
                with pe.Fori(0, TCH - 2) as c:
                    collect(i * TCH + c, True)
                for c in (TCH - 2, TCH - 1):
                    collect(i * TCH + c, False)
                pe.wait_ge(nf_d.sem, nf_d.at(i))
                nc.tensor.transpose(ps[0:1, 6, 0:PP], near[0:PP, 1:2], ident[0:PP, 0:PP]).then_inc(nf_p.sem, 1)
                with pe.If(is_far(pe, i)):
                    pe.wait_ge(f_x, 16)
                    for k in range(CHUNKS):
                        nc.tensor.matmul(ps[:, k, 0:CH], w0s[:, :], x[:, k * CH:(k + 1) * CH], start=True, stop=True
                                         ).then_inc(f_l, 1)
                    with pe.Fori(0, TCH) as c:
                        pe.wait_ge(f_a, c * 3 + 1)
                        for t in range(T4):
                            mm = nc.tensor.matmul(ps[0:PP, t, 0:OFFS], gc[:, t * PP:(t + 1) * PP], offw[:, :],
                                                  start=True, stop=True)
                        mm.then_inc(f_p, 1)
                        pe.wait_ge(f_d, c * 3 + 3)
                        for t in range(T4):
                            mm = nc.tensor.transpose(ps[:, 4, t * PP:(t + 1) * PP], acc[0:PP, t * C:(t + 1) * C],
                                                     ident[0:PP, 0:PP])
                        mm.then_inc(f_p, 1)
                        pe.wait_ge(f_a, c * 3 + 3)
                        nc.tensor.matmul(ps[:, 5, 0:T4 * PP], outw[:, :], dc, start=True, stop=True).then_inc(f_p, 1)
                gn_group(pe, i, 1)
                with pe.Fori(0, NWY) as b:
                    ib = i * NWY + b

                    def scores(pr):
                        pe.wait_ge(s_s.sem, s_s.after(ib * 4 + pr))
                        for o, h, m, r in heads():
                            for wi in range(2):
                                w = (2 * pr + wi) * NTOK
                                mm = nc.tensor.matmul(ps[wi * SLOT:(wi + 1) * SLOT, r, m * NTOK:(m + 1) * NTOK],
                                                      qk[32 * r:32 * r + 32, m, w:w + SLOT],
                                                      qk[32 * r:32 * r + 32, 4 + m, w:w + NTOK],
                                                      start=True, stop=True, skip_group_check=True)
                        mm.then_inc(s_p.sem, 1)

                    pe.wait_ge(xw_s.sem, xw_s.after(ib + 1))
                    pe.wait_ge(tr_a.sem, tr_a.at(ib, 0))
                    pe.wait_ge(tr_d.sem, tr_d.at(ib, 0))
                    pe.wait_ge(rs_s.sem, rs_s.after((i + 1) * TCH))
                    for m in range(8):
                        if m >= 2:
                            own = qk_a if m % 2 == 0 else qk_d
                            pe.wait_ge(own.sem, own.at(ib, m // 2))
                        nc.tensor.matmul(ps[:, 4 + m % 2, 0:NWY * NTOK], wqk[:, m * C:(m + 1) * C], xwb[:, :, 0:NTOK],
                                         start=True, stop=True).then_inc(qk_p.sem, 1)
                    pe.wait_ge(o_s.sem, o_s.at(ib, 0))
                    for pr in range(4):
                        if pr >= 2:
                            pe.wait_ge(v_s.sem, v_s.at(ib, pr - 1))
                        for wi in range(2):
                            for half in range(2):
                                mm = nc.tensor.matmul(ps[half * SLOT:(half + 1) * SLOT, 6 + pr % 2,
                                                         wi * 256:(wi + 1) * 256], xwb[:, 2 * pr + wi, :],
                                                      wv[:, :].rearrange("c (a p n) -> c p a n", a=2, p=2)[:, half],
                                                      start=True, stop=True, skip_group_check=True)
                        mm.then_inc(v_p.sem, 1)
                    pe.wait_ge(qk_a.sem, qk_a.at(ib))
                    pe.wait_ge(qk_d.sem, qk_d.at(ib))
                    scores(0)
                    pe.wait_ge(v_s.sem, v_s.at(ib))
                    pe.wait_ge(v_one.sem, v_one.at(i))
                    for pr in range(4):
                        u = pr % 2
                        if pr < 3:
                            scores(pr + 1)
                        pe.wait_ge(ex_s.sem, ex_s.at(ib, pr + 1))
                        for q, own in enumerate((tr_a, tr_d)):
                            pe.wait_ge(own.sem, own.at(ib, pr))
                            for k in range(4):
                                mm = nc.tensor.transpose(ps[:, 4 + q, k * C:(k + 1) * C],
                                                         e_sb[u][:, 8 * q + 2 * k:8 * q + 2 * k + 2, :], ident)
                            mm.then_inc(tr_p.sem, 1)
                        pe.wait_ge(tr_a.sem, tr_a.at(ib, pr + 1))
                        pe.wait_ge(tr_d.sem, tr_d.at(ib, pr + 1))
                        pe.wait_ge(o_s.sem, o_s.at(ib, pr))
                        alone(pe)
                        for r in range(4):
                            for k in range(2):
                                for wi in range(2):
                                    at = (2 * r + k) * C + wi * SLOT
                                    mm = nc.tensor.matmul(ps[wi * SLOT:(wi + 1) * SLOT, 6 + k,
                                                             2 * r * VD:2 * (r + 1) * VD], et[u][:, at:at + SLOT],
                                                          v_sb[pr][:, wi * 8 + k * 4 + r, :],
                                                          start=True, stop=True, skip_group_check=True)
                        mm.then_inc(pv_p.sem, 1)
                pe.wait_ge(tk_g.sem, tk_g.at(i))
                for kk in range(2):
                    mm = nc.tensor.transpose(ps[:, 0, kk * C:(kk + 1) * C], tok[:, kk * C:(kk + 1) * C], ident)
                mm.then_inc(gt_p.sem, 1)
                pe.wait_ge(gt_s.sem, gt_s.at(i))
                pe.wait_ge(wq_in.sem, wq_in.at(i))
                for oc in range(8):
                    for kc in range(4):
                        mm = nc.tensor.matmul(ps[:, 1, oc * SLOT:(oc + 1) * SLOT], wqk2[:, kc, oc * C:(oc + 1) * C],
                                              gfT[:, kc, :], start=(kc == 0), stop=(kc == 3), skip_group_check=True)
                mm.then_inc(q2_p.sem, 1)
                pe.wait_ge(q2_s.sem, q2_s.at(i))
                for o, hh, kk, r in heads2():
                    m = 2 * hh + kk
                    mm = nc.tensor.matmul(ps[hh * SLOT:(hh + 1) * SLOT, r, kk * SLOT:(kk + 1) * SLOT],
                                          qk2[32 * r:32 * r + 32, m, :], qk2[32 * r:32 * r + 32, 4 + m, :],
                                          start=True, stop=True, skip_group_check=True)
                mm.then_inc(s2_p.sem, 1)
                pe.wait_ge(a2_s.sem, a2_s.at(i))
                for o in range(8):
                    mm = nc.tensor.transpose(ps[:, 4 + o // 4, (o % 4) * C:(o % 4 + 1) * C], a2[:, o, :], ident)
                mm.then_inc(a2_p.sem, 1)
                pe.wait_ge(a2_t.sem, a2_t.at(i))
                alone(pe)

                def aggregate(nb):
                    if nb:
                        pe.wait_ge(ag_a.sem, ag_a.at(i, nb))
                        pe.wait_ge(ag_d.sem, ag_d.at(i, nb))
                        alone(pe)
                    for j in range(WS):
                        for o, hh, kk, r in heads2():
                            c0 = (4 * kk + r) * DH
                            mm = nc.tensor.matmul(ps[32 * r:32 * r + 32, 2 * hh + kk, j * SLOT:(j + 1) * SLOT],
                                                  wf[hh * SLOT:(hh + 1) * SLOT, 1 + nb * WS + j, c0:c0 + DH],
                                                  at2[hh * SLOT:(hh + 1) * SLOT, o * C + hh * SLOT:o * C + (hh + 1) * SLOT],
                                                  start=True, stop=True, skip_group_check=True)
                    mm.then_inc(ag_p.sem, 1)

                aggregate(0)
                for nb in range(WS):
                    pe.wait_ge(ag_a.sem, ag_a.at(i, nb + 1))
                    pe.wait_ge(ag_d.sem, ag_d.at(i, nb + 1))
                    if nb >= 2:
                        pe.wait_ge(y2_e.sem, y2_e.at(i, nb - 1))
                    for m in range(4):
                        mm = nc.tensor.matmul(ps[:, 4 + nb % 2, 0:WS * SLOT], wout[:, m, :], ag[:, m, :],
                                              start=(m == 0), stop=(m == 3))
                    mm.then_inc(y2_p.sem, 1)
                    if nb + 1 < WS:
                        aggregate(nb + 1)
                gn_group(pe, i, 2)
                pe.wait_ge(rl_s.sem, rl_s.at(i))
                for k in range(CHUNKS):
                    conv3(pe, k, convw, P9, c3_p)

        def gn_sqrt(act, i, g):
            o = 10 * g
            act.wait_ge(gn_var.sem, gn_var.at(i, g + 1))
            nc.scalar.activation(sm[:, o + 7:o + 8], sm[:, o + 6:o + 7], ACT.Sqrt, bias=eps_col[:, :], scale=-1.0
                                 ).then_inc(gn_sd.sem, 1)

        @block.scalar
        def _(act):
            act.wait_ge(s_init, INITS)
            act.wait_ge(s_w, WEIGHTS)
            alone(act)
            with act.Fori(0, N // 2) as i:
                for u in range(2):
                    act.wait_ge(a_var.sem, a_var.after(i * 2 + u + 1))
                    nc.scalar.activation(gm0[u][:, 3:4], gm0[u][:, 2:3], ACT.Sqrt, bias=eps_col[:, :], scale=-1.0
                                         ).then_inc(a_sd.sem, 1)
            with act.Fori(0, L) as j:
                act.wait_ge(p_ls.sem, p_ls.at(j))
                nc.scalar.activation(it[:, 12:13], it[:, 11:12], ACT.Sqrt).then_inc(p_sd.sem, 1)
            own, ownc = Chain(act, t_smp), Chain(act, t_chk)
            with act.Fori(0, N) as i:
                own.turn(i, ACT_SMP)
                gn_sqrt(act, i, 0)
                act.wait_ge(gn_ab.sem, gn_ab.at(i, 1))
                act.wait_ge(pr_s.sem, pr_s.at(i * TCH, 0))
                nc.scalar.activation(sd, x[:, :], ACT.Identity, bias=sm[:, 9:10], scale=sm[:, 8:9])
                nc.scalar.activation(vp_in, x_yx, ACT.Identity, bias=sm[:, 9:10], scale=sm[:, 8:9]
                                     ).then_inc(v1_in.sem, 1)
                for t in range(CHUNKS + 2):
                    if t < CHUNKS:
                        act.wait_ge(dw_p.sem, dw_p.at(i, t + 1))
                        nc.scalar.activation(y1[:, t * CH:(t + 1) * CH], ps[:, t, 0:CH], ACT.Identity, bias=dwb
                                             ).then_inc(dw_s.sem, 1)
                    k = t - 1
                    if 0 <= k < CHUNKS:
                        act.wait_ge(ln_c.sem, ln_c.at(i, k + 1))
                        if k >= 2:
                            act.wait_ge(ln_v.sem, ln_v.at(i, k - 1))
                        nc.scalar.activation(sq[k % 2], y1[:, k * CH:(k + 1) * CH], ACT.Square).then_inc(ln_q.sem, 1)
                    k = t - 2
                    if 0 <= k < CHUNKS:
                        act.wait_ge(ln_v.sem, ln_v.at(i, k + 1))
                        nc.scalar.activation(sd[:, k * CH:(k + 1) * CH], ps[:, k, 0:CH], ACT.Sqrt,
                                             bias=eps_col[:, :]).then_inc(ln_s.sem, 1)
                for k in range(CHUNKS):
                    act.wait_ge(ln_y.sem, ln_y.at(i, k + 1))
                    ins = nc.scalar.activation(y1[:, k * CH:(k + 1) * CH], y1[:, k * CH:(k + 1) * CH], ACT.Gelu,
                                               bias=lnb, scale=lng)
                own.step(ins)

                def fetch(ic, c):
                    act.wait_ge(of_p.sem, of_p.after(ic))
                    nc.scalar.activation(gc.rearrange("c (t p) -> c t p", t=T4),
                                         y1_tile[:, c, :, :].rearrange("c k t p -> c (k t) p"), ACT.Copy
                                         ).then_inc(gc_s.sem, 1)

                def prepare(ic):
                    ownc.turn(ic, ACT_CHK)
                    act.wait_ge(of_s.sem, of_s.after(ic + 1))
                    act.wait_ge(k_s.sem, k_s.after(ic))
                    h = [hat[0:PP, k, :, :].rearrange("p c n -> p (c n)") for k in range(3)]
                    ownc.step(nc.scalar.activation(h[1], om[0:PP, 0:2 * HN], ACT.Abs))
                    nc.scalar.activation(h[2], om[0:PP, 0:2 * HN], ACT.Relu)
                    nc.scalar.activation(h[0], om[0:PP, 0:2 * HN], ACT.Relu, scale=-1.0)
                    nc.scalar.activation(h[1], h[1], ACT.Copy, scale=-1.0, bias=1.0).then_inc(ht_s.sem, 1)
                    act.wait_ge(mk_m.sem, mk_m.after(ic + 1))
                    nc.scalar.activation(om[0:PP, 2 * HN:], om[0:PP, 2 * HN:], ACT.Exp).then_inc(mk_e.sem, 1)

                def finish(ic):
                    act.wait_ge(pr_u.sem, pr_u.at(ic))
                    act.wait_ge(sum_t.sem, sum_t.after(ic))
                    nc.scalar.activation(total[0:PP, :], ps[0:PP, 4, :], ACT.Copy).then_inc(sum_s.sem, 1)
                    act.wait_ge(sum_t.sem, sum_t.after(ic + 1))
                    act.wait_ge(oo_p.sem, oo_p.after(ic))
                    nc.scalar.activation(dc, ps[:, 6, 0:T4 * PP], ACT.Copy).then_inc(dc_s.sem, 1)
                    act.wait_ge(oo_p.sem, oo_p.after(ic + 1))
                    act.wait_ge(rs_a.sem, rs_a.at(ic, 0))
                    nc.scalar.activation(res1, ps[:, 5, 0:T4 * PP], ACT.Identity, bias=outb).then_inc(rs_s.sem, 1)

                fetch(i * TCH, slice(0, 1))
                fetch(i * TCH + 1, slice(1, 2))
                prepare(i * TCH)
                with act.Fori(0, TCH - 2) as c:
                    prepare(i * TCH + c + 1)
                    fetch(i * TCH + c + 2, bass.ds(c + 2, 1))
                    finish(i * TCH + c)
                prepare(i * TCH + TCH - 1)
                for c in (TCH - 2, TCH - 1):
                    finish(i * TCH + c)
                with act.If(is_far(act, i)):
                    with act.Fori(0, TCH) as c:
                        act.wait_ge(f_d, c * 3 + 1)
                        nc.scalar.activation(gc.rearrange("c (t p) -> c t p", t=T4),
                                             y1_tile[:, bass.ds(c, 1), :, :].rearrange("c k t p -> c (k t) p"),
                                             ACT.Copy).then_inc(f_a, 1)
                        act.wait_ge(f_d, c * 3 + 2)
                        nc.scalar.activation(om[0:PP, 2 * HN:], om[0:PP, 2 * HN:], ACT.Exp).then_inc(f_a, 1)
                        act.wait_ge(f_p, c * 3 + 2)
                        nc.scalar.activation(dc, ps[:, 4, 0:T4 * PP], ACT.Copy).then_inc(f_a, 1)
                gn_sqrt(act, i, 1)
                act.wait_ge(gn_ab.sem, gn_ab.at(i, 2))
                act.wait_ge(l2_z.sem, l2_z.at(i, 2))
                nc.scalar.activation(xwb[:, :, 0:1].rearrange("c w s -> c (w s)"), ident[:, 0:NWY], ACT.Identity,
                                     bias=wtok, scale=0.0)
                with act.Fori(0, NWY) as b:
                    ib = i * NWY + b

                    def exps(pr):
                        u = pr % 2
                        if pr < 2:
                            act.wait_ge(l2_z.sem, l2_z.at(i, 3 + pr))
                        act.wait_ge(s_s.sem, s_s.at(ib, pr + 1))
                        act.wait_ge(tr_p.sem, tr_p.at(ib, 2 * (pr - 1) if pr >= 2 else 0))
                        nc.scalar.activation(e_sb[u][:, :, 0:NTOK], ss[u].rearrange("p (o j) -> p o j", o=NH),
                                             ACT.Exp, scale=SCALE).then_inc(ex_s.sem, 1)

                    act.wait_ge(v_p.sem, v_p.at(ib, 0))
                    nc.scalar.activation(xwb[:, :, 1:NTOK].rearrange("c w (i j) -> c w i j", i=WS),
                                         x_win[:, bass.ds(b, 1)].rearrange("c a i Y j -> c (a Y) i j"),
                                         ACT.Identity, bias=sm[:, 19:20], scale=sm[:, 18:19]).then_inc(xw_s.sem, 1)
                    for m in range(0, 8, 2):
                        act.wait_ge(qk_p.sem, qk_p.at(ib, m + 1))
                        act.wait_ge(s_p.sem, s_p.at(ib, 0))
                        nc.scalar.activation(qk[:, m, 0:NWY * NTOK], ps[:, 4, 0:NWY * NTOK], ACT.Copy
                                             ).then_inc(qk_a.sem, 1)
                    for pr in range(4):
                        act.wait_ge(v_p.sem, v_p.at(ib, pr + 1))
                        act.wait_ge(pv_p.sem, pv_p.at(ib, 0))
                        if pr == 0:
                            act.wait_ge(l2_z.sem, l2_z.at(i, 5))
                        for half in range(2):
                            rows = slice(half * SLOT, (half + 1) * SLOT)
                            ins = nc.scalar.activation(v_sb[pr][rows, :, half * VD:half * VD + DH],
                                                       ps[rows, 6 + pr % 2, :].rearrange("p (k d) -> p k d", k=NH),
                                                       ACT.Copy)
                        ins.then_inc(v_s.sem, 1)
                    exps(0)
                    for pr in range(4):
                        u = pr % 2
                        act.wait_ge(pv_p.sem, pv_p.at(ib, pr - 1 if pr >= 2 else 0))
                        act.wait_ge(tr_p.sem, tr_p.at(ib, 2 * pr + 1))
                        nc.scalar.activation(et[u][:, 0:512], ps[:, 4, :], ACT.Copy).then_inc(tr_a.sem, 1)
                        if pr < 3:
                            exps(pr + 1)
                act.wait_ge(tk_v.sem, tk_v.at(i))
                nc.scalar.activation(t8[2], t8[1], ACT.Sqrt, bias=eps_col[:, :], scale=1.0 / DH).then_inc(tk_sd.sem, 1)
                act.wait_ge(tk_s.sem, tk_s.at(i))
                nc.scalar.activation(tok, tok, ACT.Gelu).then_inc(tk_g.sem, 1)
                act.wait_ge(s2_m.sem, s2_m.at(i))
                nc.scalar.activation(s2, s2, ACT.Exp, scale=SCALE).then_inc(s2_e.sem, 1)
                act.wait_ge(a2_p.sem, a2_p.at(i))
                nc.scalar.activation(at2.rearrange("p (a n) -> p a n", a=2), ps[:, 4:6, :], ACT.Copy
                                     ).then_inc(a2_t.sem, 1)
                for nb in range(WS + 1):
                    if nb < WS:
                        act.wait_ge(ag_p.sem, ag_p.at(i, nb + 1))
                        act.wait_ge(y2_p.sem, y2_p.at(i, nb))
                        nc.scalar.activation(ag[:, 0:2, :], ps[:, 0:2, 0:WS * SLOT], ACT.Copy).then_inc(ag_a.sem, 1)
                    if nb:
                        act.wait_ge(y2_p.sem, y2_p.at(i, nb))
                        act.wait_ge(y2_s.sem, y2_s.at(i, nb - 1))
                        nc.scalar.activation(yt, ps[:, 4 + (nb - 1) % 2, 0:WS * SLOT], ACT.Identity, bias=bout
                                             ).then_inc(y2_e.sem, 1)
                gn_sqrt(act, i, 2)
                act.wait_ge(gn_ab.sem, gn_ab.at(i, 3))
                nc.scalar.activation(vp_in, x_yx, ACT.Identity, bias=sm[:, 29:30], scale=sm[:, 28:29]
                                     ).then_inc(v3_s.sem, 1)
                act.wait_ge(mk_s.sem, mk_s.at(i))
                nc.scalar.activation(vp_in, mk, ACT.Relu).then_inc(rl_s.sem, 1)
                for k in range(CHUNKS):
                    act.wait_ge(c3_s.sem, c3_s.at(i, k + 1))
                    act.dma_start(a["out"][bass.ds(i, 1), :, k * CH:(k + 1) * CH].rearrange("a c n -> c (a n)"),
                                  x[:, k * CH:(k + 1) * CH]).then_inc(x_out.sem, 16)
            own.end()
            ownc.end()

        @block.vector
        def _(dve):
            V = nc.vector
            own = Chain(dve, d_init)
            own.turn(0, 3)
            dve.wait_ge(s_init, INITS)
            dve.wait_ge(s_w, WEIGHTS)
            for tap in range(P9):
                ins = V.tensor_scalar(dwdiag[:, tap, :], ident, dww[:, tap:tap + 1], None, ALU.mult)
            ins.then_inc(s_dw, 1)
            own.step(V.tensor_scalar(keep, filt, 1.0, None, ALU.is_equal))
            own.step(V.tensor_scalar(neg_mw, mw, keep, -1.0, ALU.mult, ALU.mult))
            own.step(V.tensor_scalar(floor2, keep, -2.0, None, ALU.mult))
            own.end()
            own = Chain(dve, d_a)
            with dve.Fori(0, N // 2) as i:
                own.turn(i, DVE_A)
                for u in range(2):
                    n = i * 2 + u
                    g, m = gs[u], gm0[u]
                    dve.wait_ge(a_gram[u].sem, a_gram[u].after(i + 1))
                    own.step(V.tensor_copy(g, ps[:, u, 0:C + 1]))
                    own.step(V.tensor_tensor(junk, g[:, 0:C], ident, ALU.mult))
                    own.step(V.tensor_reduce(st0[u][:, 0:1], junk, AX.X, ALU.add))
                    own.step(V.tensor_copy(st0[u][:, 1:2], g[:, C:C + 1]))
                    V.tensor_scalar(st0[u], st0[u], 1.0 / PIX, None, ALU.mult).then_inc(a_cols.sem, 1)
                    dve.wait_ge(a_gm.sem, a_gm.after(n + 1))
                    own.step(V.tensor_copy(m[:, 0:2], ps[:, 2, 0:2]))
                    own.step(V.scalar_tensor_tensor(m[:, 2:3], m[:, 1:2], m[:, 1:2], m[:, 0:1], ALU.mult, ALU.subtract))
                    V.tensor_scalar(m[:, 2:3], m[:, 2:3], 0.0, None, ALU.min).then_inc(a_var.sem, 1)
                    dve.wait_ge(a_sd.sem, a_sd.after(n + 1))
                    own.step(V.reciprocal(m[:, 4:5], m[:, 3:4]))
                    V.tensor_copy(r0[:, bass.ds(n, 1)], m[:, 4:5])
                    own.step(V.tensor_scalar(u0[:, bass.ds(n, 1)], g[:, C:C + 1], m[:, 4:5], None, ALU.mult))
                    own.step(V.tensor_scalar(q0[:, bass.ds(n, 1)], m[:, 1:2], m[:, 4:5], None, ALU.mult))
                    V.tensor_scalar(gdr[u], ident, m[:, 4:5], None, ALU.mult).then_inc(a_dr.sem, 1)
                    dve.wait_ge(a_scaled.sem, a_scaled.after(n + 1))
                    own.step(V.scalar_tensor_tensor(cacc, ps[:, 3, 0:C], m[:, 4:5], cacc, ALU.mult, ALU.add))
            own.end()
            own = Chain(dve, d_cov)
            own.turn(0, DVE_COV)
            own.step(V.scalar_tensor_tensor(wu0, q0[:, :], float(PIX), u0, ALU.mult, ALU.subtract))
            own.step(V.tensor_reduce(mu0[:, :], wu0, AX.X, ALU.add))
            V.tensor_scalar(mu0[:, :], mu0[:, :], -1.0 / (N * PIX), None, ALU.mult).then_inc(c_d, 1)
            dve.wait_ge(c_p, 1)
            own.step(V.tensor_copy(colT[0:N, :], ps[0:N, 4, 0:3 * C]))
            own.step(V.tensor_scalar(rowT[0:N, 0:C], colT[0:N, C:2 * C], -1.0, None, ALU.mult))
            own.step(V.tensor_copy(junk[0:1, :], ps[0:1, 4, 3 * C:4 * C]))
            V.tensor_scalar(rowT[0:1, C:2 * C], junk[0:1, :], -float(N * PIX), None, ALU.mult).then_inc(c_d, 1)
            dve.wait_ge(c_p, 2)
            own.step(V.tensor_tensor(cacc, cacc, ps[:, 5, 0:C], ALU.add))
            own.step(V.scalar_tensor_tensor(cacc, cacc, 1.0 / (N * PIX), mask16, ALU.mult, ALU.mult))
            own.step(V.scalar_tensor_tensor(aat[:, 0:C], ident, EPS0, cacc, ALU.mult, ALU.add))
            own.step(V.tensor_copy(aat[:, C:], aat[:, 0:C]))
            own.step(V.memset(it[:, 7:8], 3e38))
            own.step(V.memset(it[:, 8:9], -3e38))
            own.step(V.memset(it[:, 9:10], 0.0))
            own.end()
            own = Chain(dve, d_pow)
            with dve.Fori(0, L) as j:
                own.turn(j, DVE_POW)
                n = [0]

                def pe_done():
                    n[0] += 1
                    dve.wait_ge(p_p.sem, p_p.at(j, n[0]))

                own.step(V.tensor_tensor(junk, aat[:, 0:C], ident, ALU.mult))
                V.tensor_reduce(it[:, 0:1], junk, AX.X, ALU.add).then_inc(p_d.sem, 1)
                pe_done()
                own.step(V.tensor_scalar(it[:, 2:3], ps[:, 0, 0:1], 1e-4, 0.25, ALU.max, ALU.mult))
                own.step(V.reciprocal(it[:, 2:3], it[:, 2:3]))
                own.step(V.tensor_copy(it[:, 20:21], vi[:, bass.ds(j, 1)]))
                V.tensor_scalar(bbt, aat, it[:, 2:3], None, ALU.mult).then_inc(p_d.sem, 1)
                pe_done()
                V.tensor_copy(b2, ps[:, 1, 0:2 * C + 1]).then_inc(p_d.sem, 1)
                pe_done()
                V.tensor_copy(b4, ps[:, 2, 0:C + 1]).then_inc(p_d.sem, 1)
                for k in range(3):
                    pe_done()
                    V.tensor_copy(it[:, 1:2], ps[:, 3, k:k + 1]).then_inc(p_d.sem, 1)
                pe_done()
                V.tensor_copy(uw[:, 0:1], ps[:, 3, 3:4]).then_inc(p_d.sem, 1)
                pe_done()
                own.step(V.tensor_copy(uw[:, 1:2], ps[:, 3, 4:5]))
                V.tensor_scalar(uwp, uw, uw[:, 0:1], None, ALU.mult)
                own.step(V.tensor_copy(ubw.rearrange("p (a n) -> p a n", a=2),
                                       uw.rearrange("p (a n) -> p a n", n=1).to_broadcast([C, 2, C])))
                V.tensor_copy(it[:, 21:22], uw[:, 0:1]).then_inc(p_d.sem, 1)
                pe_done()
                own.step(V.tensor_scalar(it[:, 3:5], ps[:, 5, 0:2], 1.0, None, ALU.mult))
                V.tensor_tensor(uwm.rearrange("p (a n) -> p a n", a=2),
                                ps[:, 4, 0:2 * C].rearrange("p (a n) -> p a n", a=2),
                                mask16.rearrange("p (a n) -> p a n", a=1).to_broadcast([C, 2, C]), ALU.mult)
                own.step(V.tensor_scalar(it[:, 5:6], it[:, 3:4], TINY, None, ALU.max))
                own.step(V.reciprocal(it[:, 5:6], it[:, 5:6]))
                own.step(V.tensor_tensor(it[:, 6:7], it[:, 4:5], it[:, 5:6], ALU.mult))
                own.step(V.tensor_tensor(it[:, 13:14], it[:, 7:8], it[:, 6:7], ALU.is_lt))
                own.step(V.tensor_tensor(it[:, 14:15], it[:, 6:7], it[:, 8:9], ALU.is_lt))
                own.step(V.tensor_tensor(it[:, 13:14], it[:, 13:14], it[:, 14:15], ALU.max))
                own.step(V.tensor_tensor(it[:, 9:10], it[:, 9:10], it[:, 13:14], ALU.max))
                own.step(V.tensor_scalar(it[:, 10:11], it[:, 9:10], -1.0, 1.0, ALU.mult, ALU.add))
                own.step(V.tensor_tensor(it[:, 15:16], it[:, 6:7], it[:, 10:11], ALU.mult))
                V.tensor_tensor(it[:, 11:12], it[:, 15:16], it[:, 9:10], ALU.add).then_inc(p_ls.sem, 1)
                own.step(V.scalar_tensor_tensor(it[:, 7:8], it[:, 7:8], it[:, 9:10], it[:, 15:16], ALU.mult, ALU.add))
                V.memset(it[:, 8:9], EPS0)
                own.step(V.tensor_tensor(it[:, 16:17], it[:, 5:6], it[:, 10:11], ALU.mult))
                own.step(V.tensor_scalar(it[:, 17:19], uw, it[:, 16:17], -1.0, ALU.mult, ALU.mult))
                V.scalar_tensor_tensor(aat[:, 0:C], uwm[:, 0:C], it[:, 18:19], aat[:, 0:C], ALU.mult, ALU.add)
                V.scalar_tensor_tensor(aat[:, C:], uwm[:, C:], it[:, 17:18], aat[:, C:], ALU.mult, ALU.add)
                dve.wait_ge(p_sd.sem, p_sd.at(j))
                own.step(V.reciprocal(it[:, 19:20], it[:, 12:13]))
                own.step(V.tensor_scalar(it[:, 19:20], it[:, 19:20], it[:, 17:18], -1.0, ALU.mult, ALU.mult))
                own.step(V.scalar_tensor_tensor(smat, uwm[:, 0:C], it[:, 19:20], smat, ALU.mult, ALU.add))
                assert n[0] == POW_P
            own.end()
            V.tensor_tensor(w0[:, :], smat, w0row, ALU.mult).then_inc(s_w0, 1)
            dve.wait_ge(s_w0, 1)
            own, ownc, ownb, owne = Chain(dve, d_smp), Chain(dve, d_chk), Chain(dve, d_blk), Chain(dve, d_end)
            ownp = Chain(dve, d_prep)

            def group_norm(i, g):
                o = 10 * g
                for k in range(CHUNKS):
                    ins = V.bn_stats(mvs[:, k, :], x[:, k * CH:(k + 1) * CH])
                owne.step(ins)
                alone(dve)
                owne.step(V.bn_aggr(sm[:, o + 1:o + 3], mvs[:, :, :].rearrange("c k s -> c (k s)")))
                V.scalar_tensor_tensor(sm[:, o:o + 1], sm[:, o + 1:o + 2], sm[:, o + 1:o + 2], sm[:, o + 2:o + 3],
                                       ALU.mult, ALU.add).then_inc(gn_st.sem, 1)
                dve.wait_ge(gn_gm.sem, gn_gm.at(i, g + 1))
                owne.step(V.tensor_copy(sm[:, o + 4:o + 6], ps[:, 7, 0:2]))
                owne.step(V.scalar_tensor_tensor(sm[:, o + 3:o + 4], sm[:, o + 5:o + 6], sm[:, o + 5:o + 6],
                                                 sm[:, o + 4:o + 5], ALU.mult, ALU.subtract))
                V.tensor_scalar(sm[:, o + 6:o + 7], sm[:, o + 3:o + 4], 0.0, None, ALU.min).then_inc(gn_var.sem, 1)
                dve.wait_ge(gn_sd.sem, gn_sd.at(i, g + 1))
                owne.step(V.reciprocal(sm[:, o + 8:o + 9], sm[:, o + 7:o + 8]))
                V.tensor_scalar(sm[:, o + 9:o + 10], sm[:, o + 5:o + 6], sm[:, o + 8:o + 9], -1.0, ALU.mult, ALU.mult
                                ).then_inc(gn_ab.sem, 1)

            def sample_anywhere():
                chunk, rows, pixel = Chain(dve, f_o), Chain(dve, f_oy), Chain(dve, f_ox)
                n64 = T4 * G1
                logits, by_tap = om[0:PP, 2 * HN:], "p (q n) -> p q n"
                dve.sem_inc(f_go, 1)
                dve.wait_ge(f_l, CHUNKS)
                dve.wait_ge(f_t, 32)
                for k in range(CHUNKS):
                    xk = x[:, k * CH:(k + 1) * CH]
                    V.scalar_tensor_tensor(xk, ps[:, k, 0:CH], sm[:, 31:32], xk, ALU.add, ALU.add)
                V.memset(first_x[0:PP, :], 0.0).then_inc(f_used, 1)
                with dve.Fori(0, TCH) as c:
                    chunk.turn(c, 12)
                    chunk.step(V.memset(acc[0:PP, :], 0.0))
                    dve.sem_inc(f_d, 1)
                    dve.wait_ge(f_p, c * 3 + 1)
                    for t in range(T4):
                        ins = V.tensor_tensor(om[0:PP, :].rearrange("p (q t g) -> p q t g", t=T4, g=G1)[:, :, t, :],
                                              ps[0:PP, t, 0:OFFS].rearrange("p (q g) -> p q g", g=G1),
                                              offb_row[:, :].rearrange("p (q g) -> p q g", g=G1), ALU.add)
                    chunk.step(ins)
                    chunk.step(V.tensor_tensor(om[0:PP, 0:2 * HN].rearrange("p (k g) -> p k g", g=G1),
                                               om[0:PP, 0:2 * HN].rearrange("p (k g) -> p k g", g=G1),
                                               at0[0:PP, :].rearrange("p (k g) -> p k g", g=1).to_broadcast(
                                                   [PP, 2 * P9 * T4, G1]), ALU.add))
                    chunk.step(V.tensor_scalar(om[0:PP, 0:HN], om[0:PP, 0:HN], first_x[0:PP, :], None, ALU.add))
                    chunk.step(V.tensor_scalar(first_x[0:PP, :], first_x[0:PP, :], float(T4), None, ALU.add))
                    chunk.step(V.tensor_reduce(mx1[0:PP, :], logits.rearrange("p (q n) -> p n q", q=P9), AX.X, ALU.max))
                    chunk.step(V.tensor_tensor(logits.rearrange(by_tap, q=P9), logits.rearrange(by_tap, q=P9),
                                               mx1[0:PP, :].rearrange("p (a n) -> p a n", a=1).to_broadcast(
                                                   [PP, P9, n64]), ALU.subtract))
                    dve.sem_inc(f_d, 1)
                    dve.wait_ge(f_a, c * 3 + 2)
                    chunk.step(V.tensor_reduce(sx1[0:PP, :], logits.rearrange("p (q n) -> p n q", q=P9), AX.X, ALU.add))
                    chunk.step(V.reciprocal(sx1[0:PP, :], sx1[0:PP, :]))
                    chunk.step(V.tensor_tensor(logits.rearrange(by_tap, q=P9), logits.rearrange(by_tap, q=P9),
                                               sx1[0:PP, :].rearrange("p (a n) -> p a n", a=1).to_broadcast(
                                                   [PP, P9, n64]), ALU.mult))
                    chunk.step(V.memset(src_y[0:PP, :], 0.0))
                    alone(dve)
                    with dve.Fori(0, H) as y:
                        cy = c * H + y
                        rows.turn(cy, 7)
                        d, m, one = dist[0:PP, :], my[0:PP, :], float(1)
                        rows.step(V.tensor_scalar(d, om[0:PP, HN:2 * HN], src_y[0:PP, :], None, ALU.subtract))
                        rows.step(V.scalar_tensor_tensor(d, d, -one, d, ALU.mult, ALU.max))
                        rows.step(V.tensor_scalar(d, d, -one, one, ALU.mult, ALU.add))
                        rows.step(V.scalar_tensor_tensor(m, d, 0.0, logits, ALU.max, ALU.mult))
                        rows.step(V.tensor_scalar(src_y[0:PP, :], src_y[0:PP, :], one, None, ALU.add))
                        for xh in range(2):
                            rows.step(V.memset(src_x[0:PP, :], float(xh * HALF)))
                            dve.wait_ge(f_row, (cy * 2 + xh + 1) * 16)
                            alone(dve)
                            with dve.Fori(0, HALF) as xx:
                                pixel.turn((cy * 2 + xh) * HALF + xx, 8)
                                pixel.step(V.tensor_scalar(d, om[0:PP, 0:HN], src_x[0:PP, :], None, ALU.subtract))
                                pixel.step(V.scalar_tensor_tensor(d, d, -one, d, ALU.mult, ALU.max))
                                pixel.step(V.tensor_scalar(d, d, -one, one, ALU.mult, ALU.add))
                                pixel.step(V.scalar_tensor_tensor(d, d, 0.0, m, ALU.max, ALU.mult))
                                pixel.step(V.tensor_reduce(mx1[0:PP, :], d.rearrange("p (q n) -> p n q", q=P9), AX.X,
                                                           ALU.add))
                                pixel.step(V.tensor_tensor(
                                    part[0:PP, :].rearrange("p (t g e) -> p t g e", t=T4, g=G1),
                                    mx1[0:PP, :].rearrange("p (t g e) -> p t g e", t=T4, e=1).to_broadcast(
                                        [PP, T4, G1, CG]),
                                    row[0:PP, bass.ds(xx, 1), :].rearrange("p a (g e) -> p a g e", g=G1).to_broadcast(
                                        [PP, T4, G1, CG]), ALU.mult))
                                pixel.step(V.tensor_tensor(acc[0:PP, :], acc[0:PP, :], part[0:PP, :], ALU.add))
                                pixel.step(V.tensor_scalar(src_x[0:PP, :], src_x[0:PP, :], one, None, ALU.add))
                            dve.sem_inc(f_used, 1)
                    dve.sem_inc(f_d, 1)
                    dve.wait_ge(f_p, c * 3 + 3)
                    xv = x_tile[:, bass.ds(c, 1), :, :].rearrange("c k t p -> c (k t) p")
                    ins = V.scalar_tensor_tensor(xv, ps[:, 5, 0:T4 * PP].rearrange("c (t p) -> c t p", t=T4), outb, xv,
                                                 ALU.add, ALU.add)
                    chunk.step(ins)
                for ch in (chunk, rows, pixel):
                    ch.end()
                for own_sem in f_all:
                    dve.sem_clear(own_sem)

            with dve.Fori(0, N) as i:
                own.turn(i, DVE_SMP)
                owne.turn(i, 15)
                own.step(V.tensor_scalar(w0s[:, :], w0[:, :], r0[:, bass.ds(i, 1)], None, ALU.mult))
                V.tensor_tensor(sm[:, 30:31], q0[:, bass.ds(i, 1)], mu0[:, :], ALU.add).then_inc(l0_w.sem, 1)
                dve.wait_ge(l0_c.sem, l0_c.at(i))
                own.step(V.tensor_tensor(sm[:, 31:32], b0, ps[:, 7, 8:9], ALU.subtract))
                dve.wait_ge(x_out.sem, x_out.at(i, 0))
                for k in range(CHUNKS):
                    dve.wait_ge(l0_y.sem, l0_y.at(i, k + 1))
                    cols_k = slice(k * CH, (k + 1) * CH)
                    ins = V.scalar_tensor_tensor(x[:, cols_k], ps[:, k, 0:CH], sm[:, 31:32], y1[:, cols_k], ALU.add,
                                                 ALU.add)
                own.step(ins)
                group_norm(i, 0)
                dve.wait_ge(z_img.sem, z_img.at(i))
                for k in range(TCH):
                    dve.wait_ge(xp_p.sem, xp_p.at(i, k + 1))
                    V.tensor_tensor(img[0:PP, 2, 2 + k * T4:2 + (k + 1) * T4, :],
                                    ps[0:PP, k, :].rearrange("p (t c) -> p t c", t=T4),
                                    inb_row[:, :].rearrange("p (a c) -> p a c", a=1).to_broadcast([PP, T4, C]),
                                    ALU.add).then_inc(xp_s.sem, 1)
                for t in range(CHUNKS + 2):
                    if t < CHUNKS:
                        dve.wait_ge(dw_s.sem, dw_s.at(i, t + 1))
                        yk = y1[:, t * CH:(t + 1) * CH].rearrange("c (h w) -> c h w", w=W)
                        for tap in range(DW_PE, P9):
                            dy, dx = tap // 3, tap % 3
                            ins = V.scalar_tensor_tensor(yk, vp[:, ROWS * t + dy:ROWS * t + dy + ROWS, dx:dx + W],
                                                         dww[:, tap:tap + 1], yk, ALU.mult, ALU.add)
                            if tap < P9 - 1:
                                own.step(ins)
                        ins.then_inc(dw_f.sem, 1)
                    k = t - 1
                    if 0 <= k < CHUNKS:
                        dve.wait_ge(ln_m.sem, ln_m.at(i, k + 1))
                        yk = y1[:, k * CH:(k + 1) * CH]
                        V.tensor_tensor(yk, yk, ps[:, k, 0:CH], ALU.subtract).then_inc(ln_c.sem, 1)
                    k = t - 2
                    if 0 <= k < CHUNKS:
                        yk, sk = y1[:, k * CH:(k + 1) * CH], sd[:, k * CH:(k + 1) * CH]
                        dve.wait_ge(ln_s.sem, ln_s.at(i, k + 1))
                        own.step(V.reciprocal(sk, sk))
                        V.tensor_tensor(yk, yk, sk, ALU.mult).then_inc(ln_y.sem, 1)
                dve.wait_ge(cp_img.sem, cp_img.at(i))
                alone(dve)
                n64 = T4 * G1
                logits = om[0:PP, 2 * HN:]
                by_tap = "p (q n) -> p q n"

                def prepare(ic):
                    ownp.turn(ic, 1)
                    dve.wait_ge(of_p.sem, of_p.after(ic + 1))
                    dve.wait_ge(ht_s.sem, ht_s.after(ic))
                    for t in range(T4):
                        ins = V.tensor_tensor(om[0:PP, :].rearrange("p (q t g) -> p q t g", t=T4, g=G1)[:, :, t, :],
                                              ps[0:PP, t, 0:OFFS].rearrange("p (q g) -> p q g", g=G1),
                                              offb_row[:, :].rearrange("p (q g) -> p q g", g=G1), ALU.add)
                    ins.then_inc(of_s.sem, 1)
                    dve.wait_ge(of_s.sem, of_s.after(ic + 1))
                    ownp.step(V.tensor_reduce(mx1[0:PP, :], logits.rearrange("p (q n) -> p n q", q=P9), AX.X, ALU.max))
                    V.tensor_tensor(logits.rearrange(by_tap, q=P9), logits.rearrange(by_tap, q=P9),
                                    mx1[0:PP, :].rearrange("p (a n) -> p a n", a=1).to_broadcast([PP, P9, n64]),
                                    ALU.subtract).then_inc(mk_m.sem, 1)

                STEPS = 14

                def build_taps(c, u, k):
                    ic = i * TCH + c
                    if k == 0:
                        ownc.turn(ic, DVE_CHK)
                        dve.wait_ge(mk_e.sem, mk_e.after(ic + 1))
                        ownc.mark(V.tensor_reduce(sx1[0:PP, :], logits.rearrange("p (q n) -> p n q", q=P9), AX.X,
                                                  ALU.add))
                        return
                    ownc.settle()
                    if k == 1:
                        ownc.mark(V.reciprocal(sx1[0:PP, :], sx1[0:PP, :]))
                    elif k == 2:
                        ownc.mark(V.tensor_tensor(logits.rearrange(by_tap, q=P9), logits.rearrange(by_tap, q=P9),
                                                  sx1[0:PP, :].rearrange("p (a n) -> p a n", a=1).to_broadcast(
                                                      [PP, P9, n64]), ALU.mult))
                        dve.wait_ge(ht_s.sem, ht_s.after(ic + 1))
                        ownc.mark(V.tensor_reduce(near[0:PP, 0:1], hat[0:PP, 1, :, :].rearrange("p c n -> p (c n)"),
                                                  AX.X, ALU.min))
                    elif k == 3:
                        ownc.mark(V.tensor_tensor(near[0:PP, 1:2], near[0:PP, 1:2], near[0:PP, 0:1], ALU.min))
                        ownc.mark(V.tensor_tensor(hat[0:PP, :, 1, :], hat[0:PP, :, 1, :],
                                                  logits.rearrange("p (a n) -> p a n", a=1).to_broadcast([PP, 3, HN]),
                                                  ALU.mult))
                    else:
                        p = k - 4
                        if p < P9:
                            ownc.mark(V.tensor_tensor(tt[p % 2][0:PP, :], hat[0:PP, p // 3, 1, :],
                                                      hat[0:PP, p % 3, 0, :], ALU.mult))
                        if p == 0:
                            dve.wait_ge(k_z.sem, k_z.at(i, c + 1))
                        else:
                            aa, bb = (p - 1) // 3, (p - 1) % 3
                            k5 = kw[u][0:PP, :].rearrange("p (y x n) -> p x y n", y=5, x=5)[:, bb:bb + 3, aa:aa + 3, :]
                            ins = V.tensor_tensor(k5, k5, tt[(p - 1) % 2][0:PP, :].rearrange(
                                "p (x y n) -> p x y n", x=3, y=3), ALU.add)
                            if p < P9:
                                ownc.mark(ins)
                            else:
                                ins.then_inc(k_s.sem, 1)

                def multiply(c, u, s):
                    ic = i * TCH + c
                    dve.wait_ge(pr_u.sem, pr_u.at(ic, s + 1 - PRODS))
                    taps = kw[u][0:PP, s * n64:(s + 1) * n64].rearrange("p (n a) -> p n a", a=1)
                    V.tensor_tensor(prod[0:PP, s % PRODS, :].rearrange("p (n e) -> p n e", e=CG),
                                    taps.to_broadcast([PP, n64, CG]),
                                    img[0:PP, s // 5, bass.ds(c * T4 + s % 5, T4), :].rearrange(
                                        "p x (g e) -> p (x g) e", e=CG), ALU.mult).then_inc(pr_s.sem, 1)

                own.step(V.memset(near[0:PP, 1:2], 1.0))
                prepare(i * TCH)
                for k in range(STEPS):
                    build_taps(0, 0, k)
                with dve.Fori(0, TCH // 2) as j:
                    for u in range(2):
                        c = j * 2 + u
                        dve.wait_ge(k_s.sem, k_s.after(i * TCH + c + 1))
                        for s in range(TAPS):
                            multiply(c, u, s)
                            if s == PREPARE_AT:
                                prepare(i * TCH + c + 1)
                            if 0 <= s - STEPS_AT < STEPS:
                                build_taps(c + 1, 1 - u, s - STEPS_AT)
                dve.wait_ge(k_s.sem, k_s.at(i * TCH + TCH, 0))
                for s in range(TAPS):
                    multiply(TCH - 1, 0, s)
                dve.wait_ge(rs_a.sem, rs_a.at(i * TCH + TCH, 0))
                V.tensor_copy(near[0:PP, 2:3], near[0:PP, 1:2]).then_inc(nf_d.sem, 1)
                dve.wait_ge(nf_p.sem, nf_p.at(i))
                own.step(V.tensor_reduce(near[0:1, 3:4], ps[0:1, 6, 0:PP], AX.X, ALU.min))
                V.tensor_scalar(far[0:1, 0:1], near[0:1, 3:4], 0.0, None, ALU.is_lt).then_inc(nf_s.sem, 1)
                with dve.If(is_far(dve, i)):
                    sample_anywhere()
                dve.sem_inc(l1_s.sem, 1)
                group_norm(i, 1)
                dve.wait_ge(l2_z.sem, l2_z.at(i, 5))
                for u in range(4):
                    for half in range(2):
                        at = half * VD + DH
                        ins = V.memset(v_sb[u][half * SLOT:(half + 1) * SLOT, :, at:at + 1], 1.0)
                ins.then_inc(v_one.sem, 1)
                with dve.Fori(0, NWY) as b:
                    ib = i * NWY + b
                    ownb.turn(ib, 8)

                    def shift(pr):
                        u = pr % 2
                        dve.wait_ge(s_p.sem, s_p.at(ib, pr + 1))
                        sv = ps[:, 0:4, 0:4 * NTOK].rearrange("p r (m j) -> p r m j", m=4)
                        ownb.step(V.tensor_reduce(mxs[u].rearrange("p (r m) -> p r m", r=4), sv, AX.X, ALU.max))
                        dve.wait_ge(ex_s.sem, ex_s.at(ib, pr - 1 if pr >= 2 else 0))
                        V.tensor_tensor(ss[u].rearrange("p (r m j) -> p r m j", r=4, m=4), sv,
                                        mxs[u].rearrange("p (r m a) -> p r m a", r=4, a=1).to_broadcast(
                                            [C, 4, 4, NTOK]), ALU.subtract).then_inc(s_s.sem, 1)

                    for m in range(1, 8, 2):
                        dve.wait_ge(qk_p.sem, qk_p.at(ib, m + 1))
                        dve.wait_ge(s_p.sem, s_p.at(ib, 0))
                        V.tensor_copy(qk[:, m, 0:NWY * NTOK], ps[:, 5, 0:NWY * NTOK]).then_inc(qk_d.sem, 1)
                    shift(0)
                    for pr in range(4):
                        u = pr % 2
                        if pr < 3:
                            shift(pr + 1)
                        dve.wait_ge(pv_p.sem, pv_p.at(ib, pr - 1 if pr >= 2 else 0))
                        dve.wait_ge(tr_p.sem, tr_p.at(ib, 2 * pr + 2))
                        V.tensor_copy(et[u][:, 512:], ps[:, 5, :]).then_inc(tr_d.sem, 1)
                        dve.wait_ge(pv_p.sem, pv_p.at(ib, pr + 1))
                        pv = ps[:, 6:8, 0:8 * (DH + 1)].rearrange("p a (h d) -> p a h d", h=8)
                        ownb.step(V.reciprocal(rec[u].rearrange("p (a h d) -> p a h d", a=2, d=1), pv[:, :, :, DH:]))
                        dve.wait_ge(wf_in[u].sem, wf_in[u].at(ib, 64 * (pr // 2)))
                        for half in range(2):
                            ins = V.tensor_tensor(
                                o_sb[u].rearrange("p (a b r d) -> p b a r d", a=2, b=2, r=4)[:, half],
                                pv[:, :, :, 0:DH].rearrange("p a (r b) d -> p b a r d", b=2)[:, half],
                                rec[u].rearrange("p (a r b d) -> p b a r d", b=2, a=2, d=1)[:, half].to_broadcast(
                                    [C, 2, 4, DH]), ALU.mult)
                        ins.then_inc(o_s.sem, 1)
                for u in range(2):
                    dve.wait_ge(wf_in[u].sem, wf_in[u].at(i * NWY + NWY, 0))

                def per_head(v):
                    return v.rearrange("p (h d) -> p h d", h=8)

                def spread(v, n):
                    return v.rearrange("p (h a) -> p h a", a=1).to_broadcast([C, 8, n])

                own.step(V.tensor_reduce(t8[0], per_head(wf[:, 0, :]), AX.X, ALU.add))
                own.step(V.tensor_scalar(t8[0], t8[0], 1.0 / DH, None, ALU.mult))
                own.step(V.tensor_tensor(per_head(tok), per_head(wf[:, 0, :]), spread(t8[0], DH), ALU.subtract))
                own.step(V.tensor_tensor(tok2, tok, tok, ALU.mult))
                V.tensor_reduce(t8[1], per_head(tok2), AX.X, ALU.add).then_inc(tk_v.sem, 1)
                dve.wait_ge(tk_sd.sem, tk_sd.at(i))
                own.step(V.reciprocal(t8[3], t8[2]))
                own.step(V.tensor_tensor(per_head(tok), per_head(tok), spread(t8[3], DH), ALU.mult))
                own.step(V.tensor_tensor(per_head(tok), per_head(tok), lnw_row[:, 0:1, :].to_broadcast([C, 8, DH]),
                                         ALU.mult))
                V.tensor_tensor(per_head(tok), per_head(tok), lnw_row[:, 1:2, :].to_broadcast([C, 8, DH]),
                                ALU.add).then_inc(tk_s.sem, 1)
                dve.wait_ge(gt_p.sem, gt_p.at(i))
                V.tensor_copy(gfT.rearrange("p (h k) w -> p k h w", h=2),
                              ps[:, 0, 0:2 * C].rearrange("p (k h w) -> p k h w", k=2, h=2)).then_inc(gt_s.sem, 1)
                dve.wait_ge(q2_p.sem, q2_p.at(i))
                V.tensor_tensor(qk2, ps[:, 1, :].rearrange("p (m w) -> p m w", m=8), spread(bqk, SLOT),
                                ALU.add).then_inc(q2_s.sem, 1)
                dve.wait_ge(s2_p.sem, s2_p.at(i))
                sv = ps[:, 0:4, 0:2 * SLOT].rearrange("p r (k w) -> p r k w", k=2)
                own.step(V.tensor_reduce(t8[4].rearrange("p (r k) -> p r k", r=4), sv, AX.X, ALU.max))
                V.tensor_tensor(s2.rearrange("p (r k w) -> p r k w", r=4, k=2), sv,
                                t8[4].rearrange("p (r k a) -> p r k a", r=4, a=1).to_broadcast([C, 4, 2, SLOT]),
                                ALU.subtract).then_inc(s2_m.sem, 1)
                dve.wait_ge(l2_z.sem, l2_z.at(i))
                dve.wait_ge(s2_e.sem, s2_e.at(i))
                own.step(V.tensor_reduce(t8[5], per_head(s2), AX.X, ALU.add))
                own.step(V.reciprocal(t8[5], t8[5]))
                for hh in range(2):
                    rows = slice(hh * SLOT, (hh + 1) * SLOT)
                    ins = V.tensor_tensor(a2[rows, :, rows], per_head(s2)[rows],
                                          t8[5][rows].rearrange("p (h a) -> p h a", a=1).to_broadcast([SLOT, 8, SLOT]),
                                          ALU.mult)
                ins.then_inc(a2_s.sem, 1)
                for nb in range(WS):
                    dve.wait_ge(ag_p.sem, ag_p.at(i, nb + 1))
                    dve.wait_ge(y2_p.sem, y2_p.at(i, nb))
                    V.tensor_copy(ag[:, 2:4, :], ps[:, 2:4, 0:WS * SLOT]).then_inc(ag_d.sem, 1)
                dve.wait_ge(y2_s.sem, y2_s.at(i))
                group_norm(i, 2)
                dve.wait_ge(v3_s.sem, v3_s.at(i))
                V.tensor_reduce(rsum[:, 0:W], vp_in, AX.X, ALU.add)
                own.step(V.tensor_reduce(rsum[:, W:], vp_in.rearrange("c h w -> c w h"), AX.X, ALU.add))
                V.tensor_reduce(sm[:, 34:35], rsum[:, 0:W], AX.X, ALU.add)
                two = "p (a n) -> p a n"
                own.step(V.tensor_tensor(rtmp.rearrange(two, a=2), rsum.rearrange(two, a=2),
                                         idx.rearrange(two, a=1).to_broadcast([C, 2, W]), ALU.mult))
                own.step(V.tensor_reduce(sm[:, 32:34], rtmp.rearrange(two, a=2), AX.X, ALU.add))
                own.step(V.tensor_scalar(sm[:, 34:35], sm[:, 34:35], 1e-9, None, ALU.max))
                own.step(V.reciprocal(sm[:, 34:35], sm[:, 34:35]))
                own.step(V.tensor_scalar(sm[:, 32:34], sm[:, 32:34], sm[:, 34:35], 1.0, ALU.mult, ALU.max))
                own.step(V.tensor_scalar(sm[:, 32:34], sm[:, 32:34], float(H), None, ALU.min))
                own.step(V.tensor_scalar(sm[:, 32:34], sm[:, 32:34], MAGIC, None, ALU.add))
                own.step(V.tensor_scalar(sm[:, 32:34], sm[:, 32:34], MAGIC, None, ALU.subtract))
                own.step(V.tensor_scalar(sm[:, 32:34], sm[:, 32:34], 2.0 / (H - 1), -1.0 - 2.0 / (H - 1), ALU.mult,
                                         ALU.add))
                V.tensor_scalar(axy[:, 0:W], pos, sm[:, 32:33], None, ALU.subtract)
                own.step(V.tensor_scalar(axy[:, W:], pos, sm[:, 33:34], None, ALU.subtract))
                own.step(V.scalar_tensor_tensor(axy, axy, -1.0, axy, ALU.mult, ALU.max))
                own.step(V.tensor_tensor(mk, axy[:, 0:W].rearrange("p (n a) -> p n a", a=1).to_broadcast([C, H, W]),
                                         axy[:, W:].rearrange("p (a n) -> p a n", a=1).to_broadcast([C, H, W]), ALU.add))
                own.step(V.tensor_scalar(mk, mk, neg_mw, floor2, ALU.mult, ALU.max))
                V.scalar_tensor_tensor(mk, mk, 1.0, vp_in, ALU.add, ALU.mult).then_inc(mk_s.sem, 1)
                for k in range(CHUNKS):
                    dve.wait_ge(c3_p.sem, c3_p.at(i, k + 1))
                    xk = x[:, k * CH:(k + 1) * CH]
                    V.scalar_tensor_tensor(xk, ps[:, k, 0:CH], cb, xk, ALU.add, ALU.add).then_inc(c3_s.sem, 1)
            for ch in (own, ownc, ownb, owne, ownp):
                ch.end()


def kernel(**inputs):
    import numpy as np
    import concourse.bacc as bacc
    from concourse.bass_utils import run_bass_kernel_spmd

    g = {k: np.asarray(v) for k, v in inputs.items()}
    x = g["x"].reshape(N, C, PIX)
    f = np.float32
    block16 = np.kron(np.eye(GROUPS0), np.ones((L, L)))
    group4 = np.kron(np.eye(C // 4), np.full((4, 4), 0.25))
    off = g["L1_conv_off_w"].reshape(C, G1, P9, 2).transpose(0, 3, 2, 1).reshape(C, 2 * P9 * G1)
    offb = g["L1_conv_off_b"].reshape(G1, P9, 2).transpose(2, 1, 0).reshape(-1)
    msk = g["L1_conv_mask_w"].reshape(C, G1, P9).transpose(0, 2, 1).reshape(C, P9 * G1)
    mskb = g["L1_conv_mask_b"].reshape(G1, P9).T.reshape(-1)
    wqk2 = g["L2_conv_w_qk"].reshape(NH, 2, DH, INNER).transpose(1, 0, 2, 3).reshape(2 * INNER, INNER)
    bqk = g["L2_conv_b_qk"].reshape(NH, 2, DH).transpose(1, 0, 2).reshape(8, C).T
    col = [g["L0_conv_bias"].reshape(C), g["L1_conv_dw_b"], g["L1_conv_ln_g"], g["L1_conv_ln_b"], g["L1_conv_out_b"],
           g["L2_conv_b_out"], g["L3_conv_bias"], g["L3_conv_mask_weight"], g["L3_conv_filter"].reshape(C),
           g["L2_conv_window_tokens"]]
    p, q, t = np.arange(PP)[:, None, None], np.arange(P9)[None, :, None], np.arange(T4)[None, None, :]
    places = np.stack([p % 2 * HALF + q // 3 - 1 + t, p // 2 + q % 3 - 1 + 0 * t], 1)
    arrays = {
        "x": x,
        "x_t": x.transpose(0, 2, 1),
        "c_mats": np.stack([np.eye(C), block16, group4, np.full((C, C), 1.0 / C)], 1).astype(f),
        "c_pos": np.broadcast_to(np.stack([np.linspace(-1, 1, H), np.arange(1, H + 1)])[None], (C, 2, W)).astype(f),
        "c_places": places.reshape(PP, 2 * P9 * T4).astype(f),
        "cols": np.concatenate([np.stack(col, 1), g["L1_conv_dw_w"].reshape(C, 9), bqk], 1),
        "v_init": g["L0_conv_v_init"].transpose(0, 2, 1).reshape(C, L),
        "w0_row": g["L0_conv_weight"].reshape(C),
        "in_w": g["L1_conv_in_w"], "out_w": g["L1_conv_out_w"],
        "offm_w": np.concatenate([off, msk], 1), "offm_b": np.concatenate([offb, mskb]),
        "in_b": g["L1_conv_in_b"],
        "wqk": g["L2_conv_w_qkv"][:2 * INNER].T, "wv": g["L2_conv_w_qkv"][2 * INNER:].T,
        "wqk2": wqk2.T.reshape(4, C, 2 * INNER).transpose(1, 0, 2),
        "wout": g["L2_conv_w_out"].T.reshape(4, C, C).transpose(1, 0, 2),
        "convw": g["L3_conv_weight"].reshape(C, C, 9).transpose(1, 2, 0),
        "ln2_w": g["L2_conv_ln_w"], "ln2_b": g["L2_conv_ln_b"],
    }
    nc = bacc.Bacc("TRN2", target_bir_lowering=False, num_devices=1)
    feed, aps = {}, {}
    for name, v in arrays.items():
        feed[f"in_{name}"] = np.ascontiguousarray(v)
        aps[name] = nc.dram_tensor(f"in_{name}", v.shape, F32, kind="ExternalInput").ap()
    aps["img_rows"] = nc.dram_tensor("img_rows", (PP, HALF, C), F32, kind="Internal").ap()
    aps["out"] = nc.dram_tensor("out_x", (N, C, PIX), F32, kind="ExternalOutput").ap()
    build(nc, aps)
    r = run_bass_kernel_spmd(nc, [feed], core_ids=[0])
    return r.results[0]["out_x"].reshape(N, C, H, W)
```
